# Optimizing a Trainium2 kernel written in Bass

```python
import numpy as np
import jax
import jax.numpy as jnp

def _softmax(x, axis=-1):
    return jax.nn.softmax(x, axis=axis)

def _gelu(x):
    return jax.nn.gelu(x, approximate=True)

def _silu(x):
    return jax.nn.silu(x)

def _sigmoid(x):
    return jax.nn.sigmoid(x)

def _layernorm(x, axis=-1, eps=1e-05):
    m = jnp.mean(x, axis=axis, keepdims=True)
    v = jnp.var(x, axis=axis, keepdims=True)
    return (x - m) / jnp.sqrt(v + eps)

def _scatter_add(tgt, idx, src, axis=0):
    return tgt.at[idx].add(src)

def _segment_sum(src, seg, n):
    return jax.ops.segment_sum(src, seg, n)
kernel_name = 'mk_sandwich_d1_jaxref_r8_a7edcb'

def setup_inputs(seed: int=0):
    np.random.seed(seed)
    _w = jnp.asarray

    def _L0_attn_setup():
        import math
        import jax, jax.numpy as jnp
        import numpy as np
        B, T, E, H, L = (2, 256, 128, 16, 128)
        key = jax.random.key(seed)
        ks = jax.random.split(key, 11)
        w = lambda k, shape: jax.random.normal(k, shape, jnp.float32) * 0.02
        return {'x': jax.random.normal(ks[0], (B, T, E), jnp.float32), 'Wq': w(ks[1], (E, E)), 'bq': jnp.zeros((E,), jnp.float32), 'Wk': w(ks[2], (E, E)), 'bk': jnp.zeros((E,), jnp.float32), 'Wv': w(ks[3], (E, E)), 'bv': jnp.zeros((E,), jnp.float32), 'Wl': w(ks[4], (E, L)), 'bl': jnp.zeros((L,), jnp.float32), 'Wo': w(ks[5], (L, E)), 'bo': jnp.zeros((E,), jnp.float32)}
    _L0_attn_in = _L0_attn_setup()

    def _L0_ffn_setup():
        import jax, jax.numpy as jnp
        import numpy as np
        DIM = 128

        def _reference_tuple_inner(x, W_r, W_k, W_v, mu_r, mu_k):
            B, T, C = x.shape
            x_prev = jnp.concatenate([jnp.zeros((B, 1, C), x.dtype), x[:, :-1, :]], axis=1)
            xr = mu_r * x + (1.0 - mu_r) * x_prev
            xk = mu_k * x + (1.0 - mu_k) * x_prev
            r = jax.nn.sigmoid(jnp.einsum('btc,dc->btd', xr, W_r))
            k = jnp.einsum('btc,dc->btd', xk, W_k)
            k_act = jnp.square(jax.nn.relu(k))
            out = r * jnp.einsum('btc,dc->btd', k_act, W_v)
            new_state = x[:, -1, :]
            return (out, new_state)
        key = jax.random.key(seed)
        ks = jax.random.split(key, 6)
        B, T, C = (8, 256, DIM)
        x = jax.random.normal(ks[0], (B, T, C), dtype=jnp.float32)
        s = 1.0 / np.sqrt(C)
        W_r = jax.random.uniform(ks[1], (C, C), jnp.float32, -s, s)
        W_k = jax.random.uniform(ks[2], (C, C), jnp.float32, -s, s)
        W_v = jax.random.uniform(ks[3], (C, C), jnp.float32, -s, s)
        mu_r = jax.random.uniform(ks[4], (C,), jnp.float32)
        mu_k = jax.random.uniform(ks[5], (C,), jnp.float32)
        return {'x': x, 'W_r': W_r, 'W_k': W_k, 'W_v': W_v, 'mu_r': mu_r, 'mu_k': mu_k}
    _L0_ffn_in = _L0_ffn_setup()
    _d = {'L0_attn_x': _L0_attn_in['x'], 'L0_attn_Wq': _L0_attn_in['Wq'], 'L0_attn_bq': _L0_attn_in['bq'], 'L0_attn_Wk': _L0_attn_in['Wk'], 'L0_attn_bk': _L0_attn_in['bk'], 'L0_attn_Wv': _L0_attn_in['Wv'], 'L0_attn_bv': _L0_attn_in['bv'], 'L0_attn_Wl': _L0_attn_in['Wl'], 'L0_attn_bl': _L0_attn_in['bl'], 'L0_attn_Wo': _L0_attn_in['Wo'], 'L0_attn_bo': _L0_attn_in['bo'], 'L0_ffn_W_r': _L0_ffn_in['W_r'], 'L0_ffn_W_k': _L0_ffn_in['W_k'], 'L0_ffn_W_v': _L0_ffn_in['W_v'], 'L0_ffn_mu_r': _L0_ffn_in['mu_r'], 'L0_ffn_mu_k': _L0_ffn_in['mu_k']}
    _x0 = _d['L0_attn_x']
    _d['L0_attn_x'] = jax.random.normal(jax.random.fold_in(jax.random.key(seed), 1), (4, 512, 128), dtype=_x0.dtype)
    del _x0
    return _d

def reference(L0_attn_x, L0_attn_Wq, L0_attn_bq, L0_attn_Wk, L0_attn_bk, L0_attn_Wv, L0_attn_bv, L0_attn_Wl, L0_attn_bl, L0_attn_Wo, L0_attn_bo, L0_ffn_W_r, L0_ffn_W_k, L0_ffn_W_v, L0_ffn_mu_r, L0_ffn_mu_k):

    def _L0_attn_ref(x, Wq, bq, Wk, bk, Wv, bv, Wl, bl, Wo, bo):
        import math
        import jax, jax.numpy as jnp
        import numpy as np
        B, T, E, H, L = (2, 256, 128, 16, 128)
        b, t, e = x.shape
        hd = e // H
        lhd = L // H
        scale = 1.0 / math.sqrt(hd)
        q = (x @ Wq + bq).reshape(b, t, H, hd).transpose(0, 2, 1, 3)
        k = ((x @ Wk + bk) @ Wl + bl).reshape(b, t, H, lhd).transpose(0, 2, 1, 3)
        v = ((x @ Wv + bv) @ Wl + bl).reshape(b, t, H, lhd).transpose(0, 2, 1, 3)
        attn = jax.nn.softmax(jnp.einsum('bhqd,bhkd->bhqk', q, k) * scale, axis=-1)
        out = jnp.einsum('bhqk,bhkd->bhqd', attn, v)
        out = out.transpose(0, 2, 1, 3).reshape(b, t, L)
        return out @ Wo + bo

    def _L0_ffn_ref(x, W_r, W_k, W_v, mu_r, mu_k):
        import jax, jax.numpy as jnp
        import numpy as np
        DIM = 128

        def _reference_tuple_inner(x, W_r, W_k, W_v, mu_r, mu_k):
            B, T, C = x.shape
            x_prev = jnp.concatenate([jnp.zeros((B, 1, C), x.dtype), x[:, :-1, :]], axis=1)
            xr = mu_r * x + (1.0 - mu_r) * x_prev
            xk = mu_k * x + (1.0 - mu_k) * x_prev
            r = jax.nn.sigmoid(jnp.einsum('btc,dc->btd', xr, W_r))
            k = jnp.einsum('btc,dc->btd', xk, W_k)
            k_act = jnp.square(jax.nn.relu(k))
            out = r * jnp.einsum('btc,dc->btd', k_act, W_v)
            new_state = x[:, -1, :]
            return (out, new_state)
        return _reference_tuple_inner(x, W_r, W_k, W_v, mu_r, mu_k)[0]
    x = L0_attn_x
    x = x + _layernorm(_L0_attn_ref(_layernorm(x, axis=-1), L0_attn_Wq, L0_attn_bq, L0_attn_Wk, L0_attn_bk, L0_attn_Wv, L0_attn_bv, L0_attn_Wl, L0_attn_bl, L0_attn_Wo, L0_attn_bo), axis=-1)
    x = x + _layernorm(_L0_ffn_ref(_layernorm(x, axis=-1), L0_ffn_W_r, L0_ffn_W_k, L0_ffn_W_v, L0_ffn_mu_r, L0_ffn_mu_k), axis=-1)
    return x

_drawn_inputs = setup_inputs


def setup_inputs(seed=0):
    import zlib

    import numpy as np

    out = dict(_drawn_inputs(seed))
    spreads = {'L0_attn_bq': (0.0, 2.0),
     'L0_attn_bk': (0.0, 2.0),
     'L0_attn_bv': (0.0, 0.1),
     'L0_attn_bl': (0.0, 0.1),
     'L0_attn_bo': (0.0, 0.1)}
    factors = {'L0_attn_Wq': 8.0, 'L0_attn_Wk': 8.0, 'L0_attn_Wv': 8.0}
    for name, (base, spread) in spreads.items():
        noise = np.random.default_rng([zlib.crc32(name.encode()), seed]).standard_normal(out[name].shape)
        drawn = base * np.exp(spread * noise) if base else spread * noise
        out[name] = jnp.asarray(drawn.astype(out[name].dtype))
    for name, factor in factors.items():
        out[name] = (out[name] * factor).astype(out[name].dtype)
    return out
```

```python
import concourse.bass as bass
from concourse import mybir
from contextlib import ExitStack


def sandwich_kernel(nc, x, Wq, bq, Wk, bk, Wv, bv, Wl, bl, Wo, bo, W_r, W_k, W_v, mu_r, mu_k, out):
    fp32 = mybir.dt.float32
    bf16 = mybir.dt.bfloat16
    ALU = mybir.AluOpType
    ACT = mybir.ActivationFunctionType
    AX = mybir.AxisListType
    ds = bass.ds

    NB, T, E = x.shape
    H = 16
    D = E // H
    P = 128
    NT = T // P
    GH = 4
    NG = H // GH
    BLK = NG * NT
    LEAD = 7
    PARTS = 3
    ROWS = PARTS * PARTS * D
    KMAX = 96
    KEXP = KMAX + PARTS
    QUAD = 32
    SCALE = float(D) ** -0.5
    EPS = 1e-5

    ctx = ExitStack()
    with ctx:
        def sb(name, shape, dt=fp32):
            return ctx.enter_context(nc.sbuf_tensor(name, shape, dt))

        def pb(name, shape, dt=fp32):
            return ctx.enter_context(nc.psum_tensor(name, shape, dt))

        def sem(name):
            return ctx.enter_context(nc.semaphore(name))

        q_scr = nc.dram_tensor("q_scr", [NB, H, PARTS, D, PARTS, T], bf16, kind="Internal").ap()
        k_scr = nc.dram_tensor("k_scr", [NB, H, D, PARTS, T], bf16, kind="Internal").ap()

        ident = sb("ident", [P, P])
        ident_b = sb("ident_b", [P, P], bf16)
        w_in = sb("w_in", [P, 9, E])
        WQ, WK, WV, WL, WO, WR, WKF, WVF = range(8)
        w_T = sb("w_T", [P, 5, E])
        T_WK, T_WV, T_WR, T_WKF, T_WVF = range(5)
        w_kl = sb("w_kl", [P, 2, E])
        vec = sb("vec", [P, 8])
        V_BQ, V_BK, V_BV, V_BL, V_MR, V_MK = range(6)
        b_kl = sb("b_kl", [P, 2])
        bvl_wide = sb("bvl_wide", [P, P])
        bo_row = sb("bo_row", [1, E])
        ones_row = sb("ones_row", [1, P])
        bout = sb("bout", [P, NT, E])
        neghalf = sb("neghalf", [P, NT])
        eps = sb("eps", [P, NT])
        one = sb("one", [P, 1])
        idle = sb("idle", [P, 1])

        x_all = sb("x_all", [P, NB, NT * E])
        st_x = sb("st_x", [P, NT, 6])
        mv_x = sb("mv_x", [P, NT, 2])
        ve_x = sb("ve_x", [P, NT])
        rs_x = sb("rs_x", [P, NT])
        xh = sb("xh", [P, NT, E])
        xhT = sb("xhT", [P, T])
        qf = sb("qf", [P, T])
        qr = sb("qr", [P, T])
        qp = sb("qp", [P, PARTS, T], bf16)
        kf = sb("kf", [P, T])
        kr = sb("kr", [P, T])
        kp = sb("kp", [P, PARTS, T], bf16)
        v_st = sb("v_st", [P, NT, H, D])

        QS = [sb(f"QS{g}", [P, GH, T], bf16) for g in range(NG)]
        KS = [sb(f"KS{g}", [P, GH, T], bf16) for g in range(NG)]
        Vg = sb("Vg", [P, NG, NT, GH, QUAD])
        mx = sb("mx", [P, 2, GH * NT])
        mr = sb("mr", [P, 2, GH * NT])
        MC = GH * NT
        mm = sb("mm", [P, P], bf16)
        mmT = sb("mmT", [PARTS * MC, P], bf16)
        pT = sb("pT", [P, 2, GH, T])
        o_sb = sb("o_sb", [P, T])
        rsum = sb("rsum", [P, NT, GH])
        oq = sb("oq", [P, NT, H, D])

        oT = sb("oT", [P, T])
        ysb = sb("ysb", [P, NT, E])
        st_y = sb("st_y", [P, NT, 6])
        mv_y = sb("mv_y", [P, NT, 2])
        ve_y = sb("ve_y", [P, NT])
        rs_y = sb("rs_y", [P, NT])
        zy = sb("zy", [P, NT, E])
        x1 = sb("x1", [P, NT, E])
        st_1 = sb("st_1", [P, NT, 6])
        mv_1 = sb("mv_1", [P, NT, 2])
        ve_1 = sb("ve_1", [P, NT])
        rs_1 = sb("rs_1", [P, NT])
        x1h = sb("x1h", [P, NT, E])
        xs = sb("xs", [P, 1 + T])
        dx = sb("dx", [P, T])
        xr = sb("xr", [P, T])
        xk = sb("xk", [P, T])
        krelu = sb("krelu", [P, T])
        kact = sb("kact", [P, T])
        er = sb("er", [P, NT * E])
        rr = sb("rr", [P, NT * E])
        f_sb = sb("f_sb", [P, NT, E])
        st_f = sb("st_f", [P, NT, 6])
        mv_f = sb("mv_f", [P, NT, 2])
        ve_f = sb("ve_f", [P, NT])
        rs_f = sb("rs_f", [P, NT])
        zf = sb("zf", [P, NT, E])
        out_sb = sb("out_sb", [P, NT, E])

        psA = pb("psA", [P, 2, 2, T])
        psB = pb("psB", [P, 2, T])
        psO = pb("psO", [P, T])
        psM = pb("psM", [P, T])
        psM_b = psM[:, :].bitcast(bf16)

        s_vec = sem("s_vec")
        s_w = [sem(f"s_w{i}") for i in range(8)]
        s_xin = [sem(f"s_xin{b}") for b in range(NB)]
        s_const = sem("s_const")
        s_ident = sem("s_ident")
        s_pad = sem("s_pad")
        s_wt = sem("s_wt")
        s_wtc = sem("s_wtc")
        s_wkl = sem("s_wkl")
        s_wklc = sem("s_wklc")
        s_bkl = sem("s_bkl")
        s_bklc = sem("s_bklc")
        s_wide = sem("s_wide")
        s_bo = sem("s_bo")
        s_boc = sem("s_boc")

        x_st = sem("x_st")
        x_ve = sem("x_ve")
        x_rs = sem("x_rs")
        x_h = sem("x_h")
        xT_rdy = sem("xT_rdy")
        xT_tak = sem("xT_tak")
        q_rdy = sem("q_rdy")
        q_tak = sem("q_tak")
        q_r1 = sem("q_r1")
        q_p1 = sem("q_p1")
        q_p2 = sem("q_p2")
        k_rdy = sem("k_rdy")
        k_tak = sem("k_tak")
        k_r1 = sem("k_r1")
        k_p1 = sem("k_p1")
        k_p2 = sem("k_p2")
        v_rdy = sem("v_rdy")
        v_tak = sem("v_tak")
        qk_wr = sem("qk_wr")
        WW = 2 * PARTS
        ld = [sem(f"ld{g}") for g in range(NG)]
        LW = 1 + PARTS
        vg_rdy = sem("vg_rdy")

        a_rdy = sem("a_rdy")
        a_max = sem("a_max")
        m_p0 = sem("m_p0")
        m_r1 = sem("m_r1")
        m_p1 = sem("m_p1")
        m_p2 = sem("m_p2")
        m_rdy = sem("m_rdy")
        m_tak = sem("m_tak")
        m_in = sem("m_in")
        b_rdy = sem("b_rdy")
        e_rdy = sem("e_rdy")
        pv_done = sem("pv_done")
        o_tak = sem("o_tak")
        on_rdy = sem("on_rdy")
        o_rec = sem("o_rec")
        on_tak = sem("on_tak")

        oT_rdy = sem("oT_rdy")
        oT_tak = sem("oT_tak")
        y_rdy = sem("y_rdy")
        y_tak = sem("y_tak")
        y_st = sem("y_st")
        y_ve = sem("y_ve")
        y_rs = sem("y_rs")
        y_z = sem("y_z")
        x1_rdy = sem("x1_rdy")
        x1_st = sem("x1_st")
        x1_ve = sem("x1_ve")
        x1_rs = sem("x1_rs")
        x1_h = sem("x1_h")
        x1T_rdy = sem("x1T_rdy")
        x1T_tak = sem("x1T_tak")
        d_rdy = sem("d_rdy")
        xk_rdy = sem("xk_rdy")
        xr_rdy = sem("xr_rdy")
        kf_rdy = sem("kf_rdy")
        kf_tak = sem("kf_tak")
        ka_rdy = sem("ka_rdy")
        r_rdy = sem("r_rdy")
        r_tak = sem("r_tak")
        r_add = sem("r_add")
        r_rec = sem("r_rec")
        f_rdy = sem("f_rdy")
        f_tak = sem("f_tak")
        f_st = sem("f_st")
        f_ve = sem("f_ve")
        f_rs = sem("f_rs")
        f_z = sem("f_z")
        out_rdy = sem("out_rdy")
        out_wr = sem("out_wr")

        JOBS = [("P", "xT", xT_tak, 1, 2), ("F", "on-1", on_tak, NG, 0), ("M", "m1", m_tak, NG, 2),
                ("P", "q", q_tak, 2, 4), ("P", "k", k_tak, 2, 4), ("F", "oT", oT_tak, 1, 0),
                ("P", "v", v_tak, 1, 2), ("F", "y", y_tak, 1, 0), ("N", "on0", on_tak, NG, 1),
                ("M", "m2", m_tak, NG, 3), ("F", "x1T", x1T_tak, 1, 0), ("N", "on1", on_tak, NG, 2),
                ("M", "m3", m_tak, NG, 4), ("F", "kf", kf_tak, 1, 0), ("F", "r", r_tak, 1, 0),
                ("F", "f", f_tak, 1, 0), ("N", "on2", on_tak, NG, 3), ("P", "m4", m_tak, NG, 5)]

        def job_before(b, job, first, last):
            have = [j for j in JOBS if not (first and j[0] == "F") and not (last and j[0] == "P")]
            at = [j[1] for j in have].index(job)
            if not at:
                return m_tak, b * NG + 1
            _, _, taken, a, c = have[at - 1]
            return taken, b * a + c

        def later(n):
            return not isinstance(n, int) or n > 0

        block = ctx.enter_context(nc.Block())

        @block.sync
        def _(sp):
            def load_x(b):
                sp.dma_start(x_all[:, b, :].rearrange("p (t c) -> p t c", t=NT),
                             x[b, :, :].rearrange("(t p) c -> p t c", p=P)).then_inc(s_xin[b], 16)

            load_x(0)
            for i, w in ((WQ, Wq), (WK, Wk), (WV, Wv), (WL, Wl)):
                sp.dma_start(w_in[:, i, :], w[:, :]).then_inc(s_w[i], 16)
            for i, v in ((V_BQ, bq), (V_BK, bk), (V_BV, bv), (V_BL, bl), (V_MR, mu_r), (V_MK, mu_k)):
                sp.dma_start(vec[:, i:i + 1], v.rearrange("(p a) -> p a", a=1)).then_inc(s_vec, 16)
            sp.dma_start(bo_row[:, :], bo.rearrange("(a n) -> a n", a=1)).then_inc(s_vec, 16)

            def write_parts(b):
                sp.wait_ge(q_p2, b + 1)
                for s in range(PARTS):
                    dst = q_scr[ds(b, 1), :, s, :, :, :].rearrange("a h d i n -> (a h) d i n")
                    head = PARTS - s
                    sp.dma_start(dst[:, :, 0:head, :], qp[:, s:PARTS, :]).then_inc(qk_wr, 16)
                    if s:
                        sp.dma_start(dst[:, :, head:PARTS, :], qp[:, 0:s, :]).then_inc(qk_wr, 16)
                sp.wait_ge(k_p2, b + 1)
                sp.dma_start(k_scr[ds(b, 1), :, :, :, :].rearrange("a h d i n -> (a h d) i n"),
                             kp[:, :, :]).then_inc(qk_wr, 16)

            def load_group(b, g):
                qsrc = q_scr[ds(b, 1), GH * g:GH * (g + 1), :, :, :, :]
                ksrc = k_scr[ds(b, 1), GH * g:GH * (g + 1), :, :, :]
                sp.dma_start(QS[g][0:ROWS, :, :],
                             qsrc.rearrange("a h s d i n -> (a s d i) h n")).then_inc(ld[g], 16)
                for s in range(PARTS):
                    r = PARTS * D * s
                    sp.dma_start(KS[g][r:r + PARTS * D, :, :],
                                 ksrc.rearrange("a h d i n -> (a d i) h n")).then_inc(ld[g], 16)

            def parts_written(b):
                sp.wait_ge(qk_wr, (b + 1) * (16 * WW))

            def put_maxima(n, g):
                sp.wait_ge(m_tak, n + 1)
                sp.dma_start(QS[g][KMAX:KEXP, :, :].rearrange("p h n -> p (h n)"),
                             mmT[:, :]).then_inc(m_in, 16)

            def store(b):
                sp.wait_ge(out_rdy, b + 1)
                sp.dma_start(out[ds(b, 1), :, :].rearrange("a (t p) c -> (a p) t c", p=P),
                             out_sb[:, :, :]).then_inc(out_wr, 16)

            for b in range(1, NB):
                load_x(b)
            write_parts(0)
            parts_written(0)
            sp.wait_ge(s_pad, 1)
            for g in range(NG):
                load_group(0, g)
            put_maxima(0, 0)

            def batch(b, first, last):
                for g in range(NG):
                    if g < NG - 1 or not last:
                        put_maxima(b * NG + (g + 1), (g + 1) % NG)
                    if g == 0 and not last:
                        write_parts(b + 1)
                        parts_written(b + 1)
                    if not last:
                        sp.wait_ge(b_rdy, b * (BLK * GH) + GH * NT * (g + 1))
                        load_group(b + 1, g)
                if not first:
                    store(b - 1)

            batch(0, True, False)
            with sp.Fori(1, NB - 1) as i:
                batch(i, False, False)
            batch(NB - 1, False, True)
            store(NB - 1)
            sp.wait_ge(out_wr, 16 * NB)

        @block.gpsimd
        def _(pool):
            steps = [0]

            def link(ins):
                steps[0] += 1
                ins.then_inc(s_const, 1)
                pool.wait_ge(s_const, steps[0])

            link(nc.gpsimd.memset(ident[:, :], 0.0))
            link(nc.gpsimd.affine_select(out=ident[:, :], in_=ident[:, :], compare_op=ALU.not_equal,
                                         fill=1.0, base=0, pattern=[[-1, P]], channel_multiplier=1))
            nc.gpsimd.tensor_copy(ident_b[:, :], ident[:, :]).then_inc(s_ident, 1)
            link(nc.gpsimd.memset(neghalf[:, :], -0.5))
            link(nc.gpsimd.memset(eps[:, :], EPS))
            link(nc.gpsimd.memset(one[:, :], 1.0))
            link(nc.gpsimd.memset(mm[:, :], 0.0))

            def copy(dst, src, free):
                return nc.gpsimd.tensor_tensor(dst, src, one[:, :].broadcast_to([P, free]), ALU.mult)

            def rstd(b, stats, ve, rs, mv, v_sem, r_sem):
                pool.wait_ge(stats, (b + 1) * (2 * NT))
                nc.gpsimd.tensor_tensor(ve[:, :], mv[:, :, 1], eps[:, :], ALU.add).then_inc(v_sem, 1)
                pool.wait_ge(v_sem, b + 1)
                nc.gpsimd.tensor_tensor(rs[:, :], ve[:, :], neghalf[:, :], ALU.pow).then_inc(r_sem, 1)

            def minus_parts(b, full, rest, parts, taken, r1, p1, p2):
                pool.wait_ge(taken, b * 2 + 2)
                nc.gpsimd.tensor_tensor(rest[:, :], full[:, :], parts[:, 0, :],
                                        ALU.subtract).then_inc(r1, 1)
                pool.wait_ge(p1, b + 1)
                nc.gpsimd.tensor_tensor(parts[:, 2, :], rest[:, :], parts[:, 1, :],
                                        ALU.subtract).then_inc(p2, 1)

            def v_group(b, g, first):
                if g == 0:
                    pool.wait_ge(v_tak, b + 1)
                if not first:
                    pool.wait_ge(pv_done, b * BLK + (NT * (g + 1) - BLK))
                nc.gpsimd.tensor_tensor(Vg[:, g, :, :, 0:D], v_st[:, :, GH * g:GH * (g + 1), :],
                                        one[:, :].unsqueeze(2).unsqueeze(3).broadcast_to([P, NT, GH, D]),
                                        ALU.mult).then_inc(vg_rdy, 1)

            def split_maxima(n, g):
                pool.wait_ge(a_max, (n + 1) * (2 * NT))
                if later(n):
                    pool.wait_ge(m_rdy, n)
                m, r = mx[:, g % 2, :], mr[:, g % 2, :]
                copy(mm[:, 0:MC], m, MC).then_inc(m_p0, 1)
                pool.wait_ge(m_p0, n + 1)
                nc.gpsimd.tensor_tensor(r, m, mm[:, 0:MC], ALU.subtract).then_inc(m_r1, 1)
                pool.wait_ge(m_r1, n + 1)
                copy(mm[:, MC:2 * MC], r, MC).then_inc(m_p1, 1)
                pool.wait_ge(m_p1, n + 1)
                nc.gpsimd.tensor_tensor(mm[:, 2 * MC:3 * MC], r, mm[:, MC:2 * MC], ALU.subtract).then_inc(m_p2, 1)

            rstd(0, x_st, ve_x, rs_x, mv_x, x_ve, x_rs)
            link(nc.gpsimd.memset(Vg[:, :, :, :, :].rearrange("p g t h c -> p (g t h c)"), 0.0))
            link(nc.gpsimd.memset(Vg[:, :, :, :, D:D + 1], 1.0))
            link(nc.gpsimd.memset(ones_row[:, :], 1.0))
            link(nc.gpsimd.memset(xs[:, 0:1], 0.0))
            minus_parts(0, qf, qr, qp, q_tak, q_r1, q_p1, q_p2)
            minus_parts(0, kf, kr, kp, k_tak, k_r1, k_p1, k_p2)
            for g in range(NG):
                v_group(0, g, True)
            split_maxima(0, 0)

            def batch(b, first, last):
                if not first:
                    v_group(b, NG - 1, False)
                if not last:
                    rstd(b + 1, x_st, ve_x, rs_x, mv_x, x_ve, x_rs)
                split_maxima(b * NG + 1, 1)
                if not last:
                    minus_parts(b + 1, qf, qr, qp, q_tak, q_r1, q_p1, q_p2)
                    minus_parts(b + 1, kf, kr, kp, k_tak, k_r1, k_p1, k_p2)
                split_maxima(b * NG + 2, 2)
                if not first:
                    rest_first(b - 1)
                if not last:
                    v_group(b + 1, 0, False)
                split_maxima(b * NG + 3, 3)
                if not first:
                    rest_second(b - 1)
                if not last:
                    v_group(b + 1, 1, False)
                    split_maxima(b * NG + 4, 0)
                if not first:
                    rest_third(b - 1)
                if not last:
                    v_group(b + 1, 2, False)
                if not first:
                    rest_last(b - 1)

            def rest_first(e):
                rstd(e, y_st, ve_y, rs_y, mv_y, y_ve, y_rs)
                pool.wait_ge(y_z, (e + 1) * NT)
                nc.gpsimd.tensor_tensor(x1[:, :, :].rearrange("p t c -> p (t c)"),
                                        x_all[:, ds(e, 1), :].rearrange("p a n -> p (a n)"),
                                        zy[:, :, :].rearrange("p t c -> p (t c)"),
                                        ALU.add).then_inc(x1_rdy, 1)
                rstd(e, x1_st, ve_1, rs_1, mv_1, x1_ve, x1_rs)

            def rest_second(e):
                pool.wait_ge(x1T_tak, e + 1)
                nc.gpsimd.tensor_tensor(dx[:, :], xs[:, 1:1 + T], xs[:, 0:T],
                                        ALU.subtract).then_inc(d_rdy, 1)

            def rest_third(e):
                pool.wait_ge(kf_tak, e + 1)
                nc.gpsimd.tensor_tensor(kact[:, :], krelu[:, :], krelu[:, :],
                                        ALU.mult).then_inc(ka_rdy, 1)

            def rest_last(e):
                rstd(e, f_st, ve_f, rs_f, mv_f, f_ve, f_rs)
                pool.wait_ge(f_z, (e + 1) * NT)
                if later(e):
                    pool.wait_ge(out_wr, e * 16)
                nc.gpsimd.tensor_tensor(out_sb[:, :, :], x1[:, :, :], zf[:, :, :],
                                        ALU.add).then_inc(out_rdy, 1)

            batch(0, True, False)
            with pool.Fori(1, NB - 1) as i:
                batch(i, False, False)
            batch(NB - 1, False, True)
            rest_first(NB - 1)
            rest_second(NB - 1)
            rest_third(NB - 1)
            rest_last(NB - 1)

        @block.scalar
        def _(act):
            for i, w in ((WO, Wo), (WR, W_r), (WKF, W_k), (WVF, W_v)):
                act.dma_start(w_in[:, i, :], w[:, :]).then_inc(s_w[i], 16)
            act.wait_ge(s_wt, 5)
            nc.scalar.copy(w_T[:, 0:4, :].rearrange("p a n -> p (a n)"), psA[:, 0, 0, :])\
                .then_inc(s_wtc, 1)
            nc.scalar.copy(w_T[:, 4, :], psA[:, 0, 1, 0:E]).then_inc(s_wtc, 1)

            def take_xT(b):
                act.wait_ge(xT_rdy, b + 1)
                if later(b):
                    act.wait_ge(v_rdy, b)
                nc.scalar.copy(xhT[:, :], psM[:, :]).then_inc(xT_tak, 1)

            def take_parts(b, full, parts, bias, ready, taken):
                act.wait_ge(ready, b + 1)
                if later(b):
                    act.wait_ge(qk_wr, b * (16 * WW))
                nc.scalar.activation(full[:, :], psM[:, :], ACT.Identity, bias=bias).then_inc(taken, 1)
                nc.scalar.activation(parts[:, 0, :], psM[:, :], ACT.Identity,
                                     bias=bias).then_inc(taken, 1)

            def take_q(b):
                take_parts(b, qf, qp, vec[:, V_BQ:V_BQ + 1], q_rdy, q_tak)

            def take_k(b):
                take_parts(b, kf, kp, b_kl[:, 0:1], k_rdy, k_tak)

            def take_v(b):
                act.wait_ge(v_rdy, b + 1)
                if later(b):
                    act.wait_ge(vg_rdy, b * NG)
                nc.scalar.copy(v_st[:, :, :, :].rearrange("p t h d -> p (t h d)"), psM[:, :])\
                    .then_inc(v_tak, 1)

            take_xT(0)
            act.wait_ge(s_vec, 16 * 7)
            take_q(0)
            act.wait_ge(s_wkl, 2)
            nc.scalar.copy(w_kl[:, :, :].rearrange("p a n -> p (a n)"), psA[:, 1, 0, 0:2 * E])\
                .then_inc(s_wklc, 1)
            act.wait_ge(s_bklc, 2)
            take_k(0)
            take_v(0)

            def take_maxima(n):
                act.wait_ge(m_rdy, n + 1)
                if later(n):
                    act.wait_ge(m_in, n * 16)
                nc.scalar.copy(mmT[:, :], psM_b[0:PARTS * MC, 0:P]).then_inc(m_tak, 1)

            def take_o(n):
                act.wait_ge(pv_done, (n + 1) * NT)
                if later(n):
                    act.wait_ge(on_rdy, n)
                nc.scalar.copy(o_sb[:, :], psO[:, :]).then_inc(o_tak, 1)

            def take_oT(e):
                act.wait_ge(oT_rdy, e + 1)
                nc.scalar.copy(oT[:, :], psM[:, :]).then_inc(oT_tak, 1)

            def take_x1T(e):
                act.wait_ge(x1T_rdy, e + 1)
                nc.scalar.copy(xs[:, 1:1 + T], psM[:, :]).then_inc(x1T_tak, 1)

            def take_kf(e):
                act.wait_ge(kf_rdy, e + 1)
                nc.scalar.activation(krelu[:, :], psM[:, :], ACT.Relu).then_inc(kf_tak, 1)

            def take_r(e):
                act.wait_ge(r_rdy, e + 1)
                nc.scalar.activation(er[:, :], psM[:, :], ACT.Exp, scale=-1.0).then_inc(r_tak, 1)

            take_maxima(0)

            def exponentials(b, n, i):
                act.wait_ge(b_rdy, b * (BLK * GH) + (n * GH + i + 1))
                if n >= 2 or later(b):
                    act.wait_ge(pv_done, b * BLK + (n - 1))
                nc.scalar.activation(pT[:, n % 2, i, :], psB[:, i % 2, :], ACT.Exp,
                                     scale=SCALE).then_inc(e_rdy, 1)

            def batch(b, first, last):
                for n in range(BLK):
                    if n == 1 and not first:
                        take_o(b * NG - 1)
                    if n % NT == 1 and n > NT:
                        take_o(b * NG + (n // NT - 1))
                    if n == 3 and not last:
                        take_q(b + 1)
                    if n == 4 and not first:
                        take_oT(b - 1)
                    if n == 9 and not first:
                        take_x1T(b - 1)
                    if n == 12 and not first:
                        take_r(b - 1)
                    if n == 15 and not last:
                        take_maxima(b * NG + NG)
                    exponentials(b, n, 0)
                    exponentials(b, n, 1)
                    if n == 1 and not last:
                        take_xT(b + 1)
                    if n == 3 and not last:
                        take_k(b + 1)
                    if n == 4 and not last:
                        take_v(b + 1)
                    if n in (2, 6, 10):
                        take_maxima(b * NG + (n // NT + 1))
                    if n == 11 and not first:
                        take_kf(b - 1)
                    exponentials(b, n, 2)
                    exponentials(b, n, 3)

            batch(0, True, False)
            with act.Fori(1, NB - 1) as i:
                batch(i, False, False)
            batch(NB - 1, False, True)
            take_o(NB * NG - 1)
            take_oT(NB - 1)
            take_x1T(NB - 1)
            take_kf(NB - 1)
            take_r(NB - 1)

        @block.vector
        def _(dve):
            for g in range(NG):
                nc.vector.memset(QS[g][64:KMAX, :, :], 0.0)
                nc.vector.memset(KS[g][KMAX:KEXP, :, :], -1.0)
                last = nc.vector.memset(KS[g][64:KMAX, :, :], 0.0)
            last.then_inc(s_pad, 1)

            def stats(src, st, mv, s):
                for t in range(NT):
                    nc.vector.bn_stats(st[:, t, :], src(t)).then_inc(s[0], 1)
                dve.wait_ge(s[0], s[1] * (2 * NT) + NT)
                nc.vector.memset(idle[:, :], 0.0)
                for t in range(NT):
                    nc.vector.bn_aggr(mv[:, t, :], st[:, t, :]).then_inc(s[0], 1)

            def x_stats(b):
                if isinstance(b, int) and b == 0:
                    dve.wait_ge(s_xin[0], 16)
                stats(lambda t: x_all[:, ds(b, 1), E * t:E * (t + 1)].rearrange("p a n -> p (a n)"),
                      st_x, mv_x, (x_st, b))

            def x_normalise(b):
                dve.wait_ge(x_rs, b + 1)
                if later(b):
                    dve.wait_ge(xT_rdy, b)
                for t in range(NT):
                    last = nc.vector.tensor_scalar(
                        xh[:, t, :], x_all[:, ds(b, 1), E * t:E * (t + 1)].rearrange("p a n -> p (a n)"),
                        mv_x[:, t, 0:1], rs_x[:, t:t + 1], ALU.subtract, ALU.mult)
                last.then_inc(x_h, 1)

            def second_part(b, rest, parts, r1, p1):
                dve.wait_ge(r1, b + 1)
                nc.vector.tensor_copy(parts[:, 1, :], rest[:, :]).then_inc(p1, 1)

            x_stats(0)
            x_normalise(0)
            dve.wait_ge(s_vec, 16 * 7)
            dve.wait_ge(s_bkl, 2)
            nc.vector.tensor_tensor(b_kl[:, 0:1], psB[:, 0, 0:1], vec[:, V_BL:V_BL + 1],
                                    ALU.add).then_inc(s_bklc, 1)
            nc.vector.tensor_tensor(b_kl[:, 1:2], psB[:, 0, 1:2], vec[:, V_BL:V_BL + 1],
                                    ALU.add).then_inc(s_bklc, 1)
            dve.wait_ge(s_bklc, 2)
            nc.vector.tensor_copy(bvl_wide[:, :], b_kl[:, 1:2].broadcast_to([P, P])).then_inc(s_wide, 1)
            second_part(0, qr, qp, q_r1, q_p1)
            second_part(0, kr, kp, k_r1, k_p1)
            dve.wait_ge(s_bo, 1)
            for t in range(NT):
                last = nc.vector.tensor_copy(bout[:, t, :], psB[:, 1, 0:E])
            last.then_inc(s_boc, 1)
            for b in range(1, NB):
                dve.wait_ge(s_xin[b], 16)

            def maxima(group, a, g, h, u, free):
                dve.wait_ge(a_rdy, a * 2 + (u + 1))
                if h == 0 and u == 0 and free:
                    dve.wait_ge(m_p2, group - 1)
                c = NT * h + 2 * u
                nc.vector.tensor_reduce(out=mx[:, g % 2, c:c + 2], in_=psA[:, u, :, :],
                                        axis=AX.X, op=ALU.max).then_inc(a_max, 1)

            def normalise(b, g, wait_oq):
                n = b * NG + g
                dve.wait_ge(on_rdy, n + 1)
                o = psM[:, :].rearrange("p (t h c) -> p t h c", t=NT, h=GH)
                nc.vector.reciprocal(rsum[:, :, :], o[:, :, :, D]).then_inc(o_rec, 1)
                dve.wait_ge(o_rec, n + 1)
                if wait_oq:
                    dve.wait_ge(oT_rdy, b)
                nc.vector.tensor_tensor(oq[:, :, GH * g:GH * (g + 1), :], o[:, :, :, 0:D],
                                        rsum[:, :, :].unsqueeze(3).broadcast_to([P, NT, GH, D]),
                                        ALU.mult).then_inc(on_tak, 1)

            for a in range(LEAD):
                for u in range(2):
                    maxima(a // GH, a, a // GH, a % GH, u, False)

            def take_y(e):
                dve.wait_ge(y_rdy, e + 1)
                nc.vector.tensor_tensor(ysb[:, :, :].rearrange("p t c -> p (t c)"), psM[:, :],
                                        bout[:, :, :].rearrange("p t c -> p (t c)"),
                                        ALU.add).then_inc(y_tak, 1)
                dve.wait_ge(y_tak, e + 1)

            def y_stats(e):
                stats(lambda t: ysb[:, t, :], st_y, mv_y, (y_st, e))

            def y_normalise(e):
                dve.wait_ge(y_rs, e + 1)
                if later(e):
                    dve.wait_ge(x1_rdy, e)
                for t in range(NT):
                    nc.vector.tensor_scalar(zy[:, t, :], ysb[:, t, :], mv_y[:, t, 0:1],
                                            rs_y[:, t:t + 1], ALU.subtract, ALU.mult).then_inc(y_z, 1)

            def x1_stats(e):
                dve.wait_ge(x1_rdy, e + 1)
                stats(lambda t: x1[:, t, :], st_1, mv_1, (x1_st, e))

            def x1_normalise(e):
                dve.wait_ge(x1_rs, e + 1)
                for t in range(NT):
                    last = nc.vector.tensor_scalar(x1h[:, t, :], x1[:, t, :], mv_1[:, t, 0:1],
                                                   rs_1[:, t:t + 1], ALU.subtract, ALU.mult)
                last.then_inc(x1_h, 1)

            def mix(e, dst, mu, s):
                dve.wait_ge(d_rdy, e + 1)
                nc.vector.scalar_tensor_tensor(out=dst[:, :], in0=dx[:, :], scalar=vec[:, mu:mu + 1],
                                               in1=xs[:, 0:T], op0=ALU.mult, op1=ALU.add).then_inc(s, 1)

            def sigmoid_sum(e):
                dve.wait_ge(r_tak, e + 1)
                nc.vector.tensor_scalar(rr[:, :], er[:, :], 1.0, None, ALU.add).then_inc(r_add, 1)
                dve.wait_ge(r_add, e + 1)

            def take_f(e):
                dve.wait_ge(f_rdy, e + 1)
                dve.wait_ge(r_rec, (e + 1) * NT)
                nc.vector.tensor_tensor(f_sb[:, :, :].rearrange("p t c -> p (t c)"), psM[:, :],
                                        er[:, :], ALU.mult).then_inc(f_tak, 1)
                dve.wait_ge(f_tak, e + 1)

            def f_stats(e):
                stats(lambda t: f_sb[:, t, :], st_f, mv_f, (f_st, e))

            def f_normalise(e):
                dve.wait_ge(f_rs, e + 1)
                if later(e):
                    dve.wait_ge(out_rdy, e)
                for t in range(NT):
                    nc.vector.tensor_scalar(zf[:, t, :], f_sb[:, t, :], mv_f[:, t, 0:1],
                                            rs_f[:, t:t + 1], ALU.subtract, ALU.mult).then_inc(f_z, 1)

            def sigmoid_part(e, t):
                nc.vector.reciprocal(er[:, E * t:E * (t + 1)], rr[:, E * t:E * (t + 1)])\
                    .then_inc(r_rec, 1)

            def batch(b, first, last):
                for n in range(BLK):
                    ahead = n + LEAD
                    g, h = ahead // GH % NG, ahead % GH
                    if n == 2 and not first:
                        normalise(b - 1, NG - 1, False)
                    if n == 5 and not first:
                        take_y(b - 1)
                    if n in (6, 10):
                        normalise(b, n // NT - 1, n == 6 and not first)
                    if n == 14:
                        if not first:
                            take_f(b - 1)
                        normalise(b, 2, False)
                    if ahead < BLK or not last:
                        maxima(b * NG + ahead // GH, b * BLK + ahead, g, h, 0, ahead >= 2 * GH or not first)
                    if n == 0 and not last:
                        x_stats(b + 1)
                    if n == 12 and not first:
                        sigmoid_sum(b - 1)
                        sigmoid_part(b - 1, 0)
                    if n == 13 and not first:
                        sigmoid_part(b - 1, 2)
                    if ahead < BLK or not last:
                        maxima(b * NG + ahead // GH, b * BLK + ahead, g, h, 1, False)
                    if n == 0 and not last:
                        x_normalise(b + 1)
                    if n == 4 and not last:
                        second_part(b + 1, qr, qp, q_r1, q_p1)
                    if n == 5:
                        if not last:
                            second_part(b + 1, kr, kp, k_r1, k_p1)
                        if not first:
                            y_stats(b - 1)
                    if n == 6 and not first:
                        y_normalise(b - 1)
                    if n == 7 and not first:
                        x1_stats(b - 1)
                    if n == 8 and not first:
                        x1_normalise(b - 1)
                    if n == 10 and not first:
                        mix(b - 1, xk, V_MK, xk_rdy)
                        mix(b - 1, xr, V_MR, xr_rdy)
                    if n == 12 and not first:
                        sigmoid_part(b - 1, 1)
                    if n == 13 and not first:
                        sigmoid_part(b - 1, 3)
                    if n == 14 and not first:
                        f_stats(b - 1)
                    if n == 15 and not first:
                        f_normalise(b - 1)

            batch(0, True, False)
            with dve.Fori(1, NB - 1) as i:
                batch(i, False, False)
            batch(NB - 1, False, True)
            e = NB - 1
            normalise(e, NG - 1, False)
            take_y(e)
            y_stats(e)
            y_normalise(e)
            x1_stats(e)
            x1_normalise(e)
            mix(e, xk, V_MK, xk_rdy)
            mix(e, xr, V_MR, xr_rdy)
            sigmoid_sum(e)
            for t in range(NT):
                sigmoid_part(e, t)
            take_f(e)
            f_stats(e)
            f_normalise(e)

        @block.tensor
        def _(pe):
            pe.wait_ge(s_ident, 1)
            for j, i in ((T_WK, WK), (T_WV, WV), (T_WR, WR), (T_WKF, WKF), (T_WVF, WVF)):
                pe.wait_ge(s_w[i], 16)
                nc.tensor.transpose(psA[:, 0, j // 4, E * (j % 4):E * (j % 4 + 1)], w_in[:, i, :],
                                    ident[:, :]).then_inc(s_wt, 1)

            def product_by_tile(lhs, rhs, ready):
                for t in range(NT):
                    last = nc.tensor.matmul(psM[:, E * t:E * (t + 1)], lhs[:, P * t:P * (t + 1)], rhs,
                                            start=True, stop=True)
                last.then_inc(ready, 1)

            def transposes(src, ready):
                for t in range(NT):
                    last = nc.tensor.transpose(psM[:, P * t:P * (t + 1)], src(t), ident[:, :])
                last.then_inc(ready, 1)

            def job_xT(e):
                pe.wait_ge(x_h, e + 1)
                transposes(lambda t: xh[:, t, :], xT_rdy)

            def job_q(e):
                pe.wait_ge(xT_tak, e + 1)
                nc.tensor.matmul(psM[:, :], w_in[:, WQ, :], xhT[:, :], start=True, stop=True)\
                    .then_inc(q_rdy, 1)

            def job_k(e):
                nc.tensor.matmul(psM[:, :], w_kl[:, 0, :], xhT[:, :], start=True, stop=True)\
                    .then_inc(k_rdy, 1)

            def job_v(e):
                product_by_tile(xhT, w_kl[:, 1, :], v_rdy)

            def job_m(n):
                pe.wait_ge(m_p2, n + 1)
                nc.tensor.transpose(psM_b[:, 0:P], mm[:, :], ident_b[:, :]).then_inc(m_rdy, 1)

            def job_on(n):
                pe.wait_ge(o_tak, n + 1)
                transposes(lambda t: o_sb[:, P * t:P * (t + 1)], on_rdy)

            def job_oT(e):
                pe.wait_ge(on_tak, (e + 1) * NG)
                transposes(lambda t: oq[:, t, :, :].rearrange("p h d -> p (h d)"), oT_rdy)

            def job_y(e):
                pe.wait_ge(oT_tak, e + 1)
                product_by_tile(oT, w_in[:, WO, :], y_rdy)

            def job_x1T(e):
                pe.wait_ge(x1_h, e + 1)
                transposes(lambda t: x1h[:, t, :], x1T_rdy)

            def job_kf(e):
                pe.wait_ge(xk_rdy, e + 1)
                nc.tensor.matmul(psM[:, :], w_T[:, T_WKF, :], xk[:, :], start=True, stop=True)\
                    .then_inc(kf_rdy, 1)

            def job_r(e):
                pe.wait_ge(xr_rdy, e + 1)
                product_by_tile(xr, w_T[:, T_WR, :], r_rdy)

            def job_f(e):
                pe.wait_ge(ka_rdy, e + 1)
                product_by_tile(kact, w_T[:, T_WVF, :], f_rdy)

            def scores_for_maxima(e, a, g, h, u, later_pair):
                if u == 0:
                    if h == 0:
                        pe.wait_ge(ld[g], (e + 1) * (16 * LW))
                if later_pair:
                    pe.wait_ge(a_max, a * 2 + (u - 1))
                for j in range(2):
                    t = 2 * u + j
                    last = nc.tensor.matmul(psA[:, u, j, :], QS[g][0:KMAX, h, P * t:P * (t + 1)],
                                            KS[g][0:KMAX, h, :], start=True, stop=True)
                last.then_inc(a_rdy, 1)

            def scores_for_exponentials(b, n, i, later_tile):
                g, t = n // NT, n % NT
                if t == 0 and i == 0:
                    pe.wait_ge(m_in, b * (16 * NG) + 16 * (g + 1))
                if later_tile:
                    pe.wait_ge(e_rdy, b * (BLK * GH) + (n * GH + i - 1))
                nc.tensor.matmul(psB[:, i % 2, :], KS[g][0:KEXP, i, P * t:P * (t + 1)],
                                 QS[g][0:KEXP, i, :], start=True, stop=True).then_inc(b_rdy, 1)

            def times_v(b, n, later_group):
                g, t = n // NT % NG, n % NT
                if t == 0:
                    pe.wait_ge(vg_rdy, b * NG + (n // NT + 1))
                    if later_group:
                        pe.wait_ge(o_tak, b * NG + n // NT)
                pe.wait_ge(e_rdy, b * (BLK * GH) + GH * (n + 1))
                for i in range(GH):
                    last = nc.tensor.matmul(psO[QUAD * i:QUAD * (i + 1), :], Vg[:, g, t, i, :],
                                            pT[:, n % 2, i, :], start=(t == 0), stop=(t == NT - 1))
                last.then_inc(pv_done, 1)

            job_xT(0)
            job_q(0)
            pe.wait_ge(s_wtc, 2)
            pe.wait_ge(s_w[WL], 16)
            for j in range(2):
                nc.tensor.matmul(psA[:, 1, 0, E * j:E * (j + 1)], w_T[:, T_WK + j, :], w_in[:, WL, :],
                                 start=True, stop=True).then_inc(s_wkl, 1)
            pe.wait_ge(s_vec, 16 * 7)
            for j in range(2):
                nc.tensor.matmul(psB[:, 0, j:j + 1], w_in[:, WL, :], vec[:, V_BK + j:V_BK + j + 1],
                                 start=True, stop=True).then_inc(s_bkl, 1)
            pe.wait_ge(s_wklc, 1)
            pe.wait_ge(q_tak, 2)
            job_k(0)
            pe.wait_ge(k_tak, 2)
            job_v(0)
            pe.wait_ge(s_wide, 1)
            pe.wait_ge(s_w[WO], 16)
            pe.wait_ge(s_const, 10)
            nc.tensor.matmul(psB[:, 1, 0:E], bvl_wide[:, :], w_in[:, WO, :], start=True, stop=False)
            nc.tensor.matmul(psB[:, 1, 0:E], ones_row[:, :], bo_row[:, :], start=False,
                             stop=True).then_inc(s_bo, 1)
            for a in range(LEAD):
                for u in range(2):
                    scores_for_maxima(0, a, a // GH, a % GH, u, a > 0)
                if a == GH:
                    pe.wait_ge(v_tak, 1)
                    job_m(0)
            pe.wait_ge(s_boc, 1)

            def batch(b, first, last):
                def job(name, do):
                    pe.wait_ge(*job_before(b, name, first, last))
                    do()

                for n in range(BLK):
                    scores_for_exponentials(b, n, 0, n > 0 or not first)
                    scores_for_exponentials(b, n, 1, n > 0 or not first)
                    if n == 1 and not last:
                        job("xT", lambda: job_xT(b + 1))
                    if n == 3 and not last:
                        job("k", lambda: job_k(b + 1))
                    if n == 4 and not last:
                        job("v", lambda: job_v(b + 1))
                    if n == 11 and not first:
                        job("kf", lambda: job_kf(b - 1))
                    if n in (2, 6, 10):
                        job(f"m{n // NT + 1}", lambda: job_m(b * NG + (n // NT + 1)))
                    if n == 14:
                        job("on2", lambda: job_on(b * NG + 2))
                    ahead = n + LEAD
                    if ahead < BLK or not last:
                        for u in range(2):
                            scores_for_maxima(b + ahead // BLK, b * BLK + ahead, ahead // GH % NG,
                                              ahead % GH, u, True)
                    scores_for_exponentials(b, n, 2, True)
                    scores_for_exponentials(b, n, 3, True)
                    if n or not first:
                        times_v_before(b, n, first)
                    if n == 1 and not first:
                        job("on-1", lambda: job_on(b * NG - 1))
                    if n == 2 and not last:
                        job("q", lambda: job_q(b + 1))
                    if n == 3 and not first:
                        job("oT", lambda: job_oT(b - 1))
                    if n == 4 and not first:
                        job("y", lambda: job_y(b - 1))
                    if n in (5, 9):
                        job(f"on{n // NT - 1}", lambda: job_on(b * NG + (n // NT - 1)))
                    if n == 8 and not first:
                        job("x1T", lambda: job_x1T(b - 1))
                    if n == 11 and not first:
                        job("r", lambda: job_r(b - 1))
                    if n == 13 and not first:
                        job("f", lambda: job_f(b - 1))
                    if n == 14 and not last:
                        job("m4", lambda: job_m(b * NG + NG))

            def times_v_before(b, n, first):
                if n:
                    times_v(b, n - 1, n > 1 or not first)
                else:
                    times_v(b - 1, BLK - 1, True)

            batch(0, True, False)
            with pe.Fori(1, NB - 1) as i:
                batch(i, False, False)
            batch(NB - 1, False, True)
            e = NB - 1
            times_v(e, BLK - 1, True)
            pe.wait_ge(on_tak, NG * e + 3)
            job_on(NG * e + 3)
            job_oT(e)
            job_y(e)
            pe.wait_ge(y_tak, e + 1)
            job_x1T(e)
            job_kf(e)
            pe.wait_ge(kf_tak, e + 1)
            job_r(e)
            pe.wait_ge(r_tak, e + 1)
            job_f(e)


_INS = ["x", "Wq", "bq", "Wk", "bk", "Wv", "bv", "Wl", "bl", "Wo", "bo"]
_FFN = ["W_r", "W_k", "W_v", "mu_r", "mu_k"]


def kernel(**inputs):
    import numpy as _np
    import concourse.bacc as _bacc
    from concourse import mybir as _mybir
    from concourse.bass_utils import run_bass_kernel_spmd as _run

    nc = _bacc.Bacc("TRN2", target_bir_lowering=False, num_devices=1)
    arrays, args = {}, []
    for name in ["L0_attn_" + n for n in _INS] + ["L0_ffn_" + n for n in _FFN]:
        a = _np.ascontiguousarray(inputs[name])
        arrays[f"in_{name}_dram"] = a
        args.append(nc.dram_tensor(f"in_{name}_dram", a.shape, _mybir.dt.from_np(a.dtype),
                                   kind="ExternalInput").ap())
    shape = inputs["L0_attn_x"].shape
    args.append(nc.dram_tensor("out_dram", shape, _mybir.dt.float32, kind="ExternalOutput").ap())
    sandwich_kernel(nc, *args)
    r = _run(nc, [arrays], core_ids=[0])
    return r.results[0]["out_dram"]
```

```python
import concourse.bass as bass
from concourse import mybir
from contextlib import ExitStack


def sandwich_kernel(nc, x, Wq, bq, Wk, bk, Wv, bv, Wl, bl, Wo, bo, W_r, W_k, W_v, mu_r, mu_k, out):
    fp32 = mybir.dt.float32
    bf16 = mybir.dt.bfloat16
    u32 = mybir.dt.uint32
    ALU = mybir.AluOpType
    ACT = mybir.ActivationFunctionType
    AX = mybir.AxisListType
    ds = bass.ds

    NB, T, E = x.shape
    H = 16
    D = E // H
    P = 128
    NT = T // P
    GH = 4
    NG = H // GH
    BLK = NG * NT
    LEAD = 6
    PARTS = 3
    ROWS = PARTS * PARTS * D
    KMAX = 96
    KEXP = KMAX + PARTS
    QUAD = 32
    SCALE = float(D) ** -0.5
    EPS = 1e-5
    MINUS_ONES = 0xBF80BF80

    ctx = ExitStack()
    with ctx:
        def sb(name, shape, dt=fp32):
            return ctx.enter_context(nc.sbuf_tensor(name, shape, dt))

        def pb(name, shape, dt=fp32):
            return ctx.enter_context(nc.psum_tensor(name, shape, dt))

        def sem(name):
            return ctx.enter_context(nc.semaphore(name))

        CYC = 2 * PARTS - 1
        q_scr = nc.dram_tensor("q_scr", [NB, CYC, D, H, T], bf16, kind="Internal").ap()
        k_scr = nc.dram_tensor("k_scr", [NB, PARTS, D, H, T], bf16, kind="Internal").ap()

        ident = sb("ident", [P, P])
        ident_b = sb("ident_b", [P, P], bf16)
        w_in = sb("w_in", [P, 9, E])
        WQ, WK, WV, WL, WO, WR, WKF, WVF = range(8)
        w_T = sb("w_T", [P, 5, E])
        T_WK, T_WV, T_WR, T_WKF, T_WVF = range(5)
        w_kl = sb("w_kl", [P, 2, E])
        vec = sb("vec", [P, 8])
        V_BQ, V_BK, V_BV, V_BL, V_MR, V_MK = range(6)
        b_kl = sb("b_kl", [P, 2])
        bvl_wide = sb("bvl_wide", [P, P])
        bo_row = sb("bo_row", [1, E])
        ones_row = sb("ones_row", [1, P])
        bout = sb("bout", [P, NT, E])
        neghalf = sb("neghalf", [P, NT])
        eps = sb("eps", [P, NT])
        one = sb("one", [P, 1])
        minus = sb("minus", [P, NT])
        idle = sb("idle", [P, 1])

        x_all = sb("x_all", [P, NB, NT * E])
        st_x = sb("st_x", [P, NB, NT, 6])
        mv_x = sb("mv_x", [P, NB, NT, 2])
        ve_x = sb("ve_x", [P, NB, NT])
        rs_x = sb("rs_x", [P, NB, NT])
        xh = sb("xh", [P, NB, NT, E])
        xhT = sb("xhT", [P, 2, T])
        qf = sb("qf", [P, T])
        qr = sb("qr", [P, T])
        qp = sb("qp", [P, 2, PARTS, T], bf16)
        kf = sb("kf", [P, T])
        kr = sb("kr", [P, T])
        kp = sb("kp", [P, 2, PARTS, T], bf16)
        v_st = sb("v_st", [P, NB, NT * H * D])

        QS = [sb(f"QS{g}", [P, GH, T], bf16) for g in range(NG)]
        KS = [sb(f"KS{g}", [P, GH, T], bf16) for g in range(NG)]
        Vg = sb("Vg", [P, NG, NT, GH, QUAD])
        mx = sb("mx", [P, 2, GH * NT])
        mr = sb("mr", [P, 2, GH * NT])
        MC = GH * NT
        mm = sb("mm", [P, P], bf16)
        mmT = sb("mmT", [PARTS * MC, P], bf16)
        pT = sb("pT", [P, 2, GH, T])
        o_sb = sb("o_sb", [P, T])
        rsum = sb("rsum", [P, NT, GH])
        oq = sb("oq", [P, NT, H, D])

        oT = sb("oT", [P, T])
        ysb = sb("ysb", [P, NT, E])
        st_y = sb("st_y", [P, NT, 6])
        mv_y = sb("mv_y", [P, NT, 2])
        ve_y = sb("ve_y", [P, NT])
        rs_y = sb("rs_y", [P, NT])
        nm_y = sb("nm_y", [P, NT])
        nb_y = sb("nb_y", [P, NT])
        zy = sb("zy", [P, NT, E])
        x1 = sb("x1", [P, NT, E])
        st_1 = sb("st_1", [P, NT, 6])
        mv_1 = sb("mv_1", [P, NT, 2])
        ve_1 = sb("ve_1", [P, NT])
        rs_1 = sb("rs_1", [P, NT])
        nm_1 = sb("nm_1", [P, NT])
        nb_1 = sb("nb_1", [P, NT])
        x1h = sb("x1h", [P, NT, E])
        xs = sb("xs", [P, 1 + T])
        dx = sb("dx", [P, T])
        xr = sb("xr", [P, T])
        xk = sb("xk", [P, T])
        krelu = sb("krelu", [P, T])
        kact = sb("kact", [P, T])
        er = sb("er", [P, NT * E])
        rr = sb("rr", [P, NT * E])
        f_sb = sb("f_sb", [P, NT, E])
        st_f = sb("st_f", [P, NT, 6])
        mv_f = sb("mv_f", [P, NT, 2])
        ve_f = sb("ve_f", [P, NT])
        rs_f = sb("rs_f", [P, NT])
        nm_f = sb("nm_f", [P, NT])
        nb_f = sb("nb_f", [P, NT])
        zf = sb("zf", [P, NT, E])
        out_sb = sb("out_sb", [P, NT, E])

        psA = pb("psA", [P, 2, 2, T])
        psB = pb("psB", [P, 2, T])
        psO = pb("psO", [P, T])
        psM = pb("psM", [P, T])
        psM_b = psM[:, :].bitcast(bf16)

        s_vec = sem("s_vec")
        s_w = [sem(f"s_w{i}") for i in range(8)]
        s_xin = [sem(f"s_xin{b}") for b in range(NB)]
        s_const = sem("s_const")
        s_ident = sem("s_ident")
        s_padp = sem("s_padp")
        s_padv = sem("s_padv")
        s_wt = sem("s_wt")
        s_wtc = sem("s_wtc")
        s_wkl = sem("s_wkl")
        s_wklc = sem("s_wklc")
        s_bkl = sem("s_bkl")
        s_bklc = sem("s_bklc")
        s_wide = sem("s_wide")
        s_bo = sem("s_bo")
        s_boc = sem("s_boc")

        x_st = sem("x_st")
        x_ve = sem("x_ve")
        x_rs = sem("x_rs")
        x_h = sem("x_h")
        xT_rdy = sem("xT_rdy")
        xT_tak = sem("xT_tak")
        q_rdy = sem("q_rdy")
        q_tak = sem("q_tak")
        q_r1 = sem("q_r1")
        q_p1 = sem("q_p1")
        q_p2 = sem("q_p2")
        k_rdy = sem("k_rdy")
        k_tak = sem("k_tak")
        k_r1 = sem("k_r1")
        k_p1 = sem("k_p1")
        k_p2 = sem("k_p2")
        v_rdy = sem("v_rdy")
        v_tak = sem("v_tak")
        qk_wr = [sem(f"qk_wr{b}") for b in range(NB)]
        WW = CYC + PARTS
        ld = [sem(f"ld{g}") for g in range(NG)]
        LW = PARTS + 1
        vg_rdy = sem("vg_rdy")

        a_rdy = sem("a_rdy")
        a_max = sem("a_max")
        m_p0 = sem("m_p0")
        m_r1 = sem("m_r1")
        m_p1 = sem("m_p1")
        m_p2 = sem("m_p2")
        m_rdy = sem("m_rdy")
        m_tak = sem("m_tak")
        m_in = sem("m_in")
        b_rdy = sem("b_rdy")
        e_rdy = sem("e_rdy")
        pv_done = sem("pv_done")
        o_tak = sem("o_tak")
        on_rdy = sem("on_rdy")
        o_rec = sem("o_rec")
        on_tak = sem("on_tak")

        oT_rdy = sem("oT_rdy")
        oT_tak = sem("oT_tak")
        y_rdy = sem("y_rdy")
        y_tak = sem("y_tak")
        y_st = sem("y_st")
        y_ve = sem("y_ve")
        y_rs = sem("y_rs")
        y_nm = sem("y_nm")
        y_nb = sem("y_nb")
        y_z = sem("y_z")
        x1_rdy = sem("x1_rdy")
        x1_st = sem("x1_st")
        x1_ve = sem("x1_ve")
        x1_rs = sem("x1_rs")
        x1_nm = sem("x1_nm")
        x1_nb = sem("x1_nb")
        x1_h = sem("x1_h")
        x1T_rdy = sem("x1T_rdy")
        x1T_tak = sem("x1T_tak")
        d_rdy = sem("d_rdy")
        xk_rdy = sem("xk_rdy")
        xr_rdy = sem("xr_rdy")
        kf_rdy = sem("kf_rdy")
        kf_tak = sem("kf_tak")
        ka_rdy = sem("ka_rdy")
        r_rdy = sem("r_rdy")
        r_tak = sem("r_tak")
        r_add = sem("r_add")
        r_rec = sem("r_rec")
        f_rdy = sem("f_rdy")
        f_tak = sem("f_tak")
        f_st = sem("f_st")
        f_ve = sem("f_ve")
        f_rs = sem("f_rs")
        f_nm = sem("f_nm")
        f_nb = sem("f_nb")
        f_z = sem("f_z")
        out_rdy = sem("out_rdy")
        out_wr = sem("out_wr")

        JOBS = [("F", "on-1", on_tak, NG, 0), ("M", "m1", m_tak, NG, 2), ("F", "oT", oT_tak, 1, 0),
                ("F", "y", y_tak, 1, 0), ("N", "on0", on_tak, NG, 1), ("M", "m2", m_tak, NG, 3),
                ("F", "x1T", x1T_tak, 1, 0), ("N", "on1", on_tak, NG, 2), ("M", "m3", m_tak, NG, 4),
                ("F", "kf", kf_tak, 1, 0), ("F", "r", r_tak, 1, 0), ("F", "f", f_tak, 1, 0),
                ("N", "on2", on_tak, NG, 3), ("L", "m4", m_tak, NG, 5)]

        def job_before(b, job, first, last):
            have = [j for j in JOBS if not (first and j[0] == "F") and not (last and j[0] == "L")]
            at = [j[1] for j in have].index(job)
            if not at:
                return m_tak, b * NG + 1
            _, _, taken, a, c = have[at - 1]
            return taken, b * a + c

        def later(n):
            return not isinstance(n, int) or n > 0

        TAIL = BLK - LEAD

        def score_bank(n, i, last):
            if last and n >= TAIL and i >= 2:
                return psA[:, 0, i - 2, :]
            return psB[:, i % 2, :]

        block = ctx.enter_context(nc.Block())

        @block.sync
        def _(sp):
            def load_x(b):
                sp.dma_start(x_all[:, b, :].rearrange("p (t c) -> p t c", t=NT),
                             x[b, :, :].rearrange("(t p) c -> p t c", p=P)).then_inc(s_xin[b], 16)

            load_x(0)
            for i, w in ((WQ, Wq), (WK, Wk), (WV, Wv), (WL, Wl)):
                sp.dma_start(w_in[:, i, :], w[:, :]).then_inc(s_w[i], 16)
            for i, v in ((V_BQ, bq), (V_BK, bk), (V_BV, bv), (V_BL, bl), (V_MR, mu_r), (V_MK, mu_k)):
                sp.dma_start(vec[:, i:i + 1], v.rearrange("(p a) -> p a", a=1)).then_inc(s_vec, 16)
            sp.dma_start(bo_row[:, :], bo.rearrange("(a n) -> a n", a=1)).then_inc(s_vec, 16)

            def write_parts(b):
                for scr, parts, slots, first, second, third in ((q_scr, qp, CYC, q_tak, q_p1, q_p2),
                                                                (k_scr, kp, PARTS, k_tak, k_p1, k_p2)):
                    for i, (made, count) in enumerate(((first, 2 * b + 2), (second, b + 1), (third, b + 1))):
                        sp.wait_ge(made, count)
                        for slot in range(i, slots, PARTS):
                            sp.dma_start(scr[b, slot, :, :, :].rearrange("d h n -> h d n"),
                                         parts[:, b % 2, i, :]).then_inc(qk_wr[b], 16)

            def load_group(b, g):
                q_src = q_scr[ds(b, 1), :, :, GH * g:GH * (g + 1), :]
                k_src = k_scr[ds(b, 1), :, :, GH * g:GH * (g + 1), :]
                for s in range(PARTS):
                    r = PARTS * D * s
                    sp.dma_start(QS[g][r:r + PARTS * D, :, :].rearrange("p h n -> p (h n)"),
                                 q_src[:, s:s + PARTS, :, :, :].rearrange("a i d h n -> (a i d) (h n)"))\
                        .then_inc(ld[g], 16)
                sp.dma_start(KS[g][0:ROWS, :, :].rearrange("p h n -> p (h n)"),
                             k_src.rearrange("a i d h n -> a (i d) (h n)")
                             .broadcast_to([PARTS, PARTS * D, GH * T])).then_inc(ld[g], 16)

            def put_maxima(n, g):
                sp.wait_ge(m_tak, n + 1)
                sp.dma_start(QS[g][KMAX:KEXP, :, :].rearrange("p h n -> p (h n)"),
                             mmT[:, :]).then_inc(m_in, 16)

            def store(b):
                sp.wait_ge(out_rdy, b + 1)
                sp.dma_start(out[ds(b, 1), :, :].rearrange("a (t p) c -> (a p) t c", p=P),
                             out_sb[:, :, :]).then_inc(out_wr, 16)

            for b in range(1, NB):
                load_x(b)
            write_parts(0)
            sp.wait_ge(qk_wr[0], 16 * WW)
            for g in range(NG):
                sp.wait_ge(s_padp, (1, 2, 5, 8)[g])
                if g < 2:
                    sp.wait_ge(s_padv, 2 * g + 2)
                load_group(0, g)
            write_parts(1)
            write_parts(2)
            put_maxima(0, 0)
            write_parts(3)
            for b in range(1, NB):
                sp.wait_ge(qk_wr[b], 16 * WW)

            def batch(b, first, last):
                for g in range(NG):
                    if g < NG - 1 or not last:
                        put_maxima(b * NG + (g + 1), (g + 1) % NG)
                    if not last:
                        sp.wait_ge(b_rdy, b * (BLK * GH) + GH * NT * (g + 1))
                        load_group(b + 1, g)
                if not first:
                    store(b - 1)

            batch(0, True, False)
            with sp.Fori(1, NB - 1) as i:
                batch(i, False, False)
            batch(NB - 1, False, True)
            store(NB - 1)
            sp.wait_ge(out_wr, 16 * NB)

        @block.gpsimd
        def _(pool):
            steps = [0]

            def link(ins):
                steps[0] += 1
                ins.then_inc(s_const, 1)
                pool.wait_ge(s_const, steps[0])

            link(nc.gpsimd.memset(ident[:, :], 0.0))
            link(nc.gpsimd.affine_select(out=ident[:, :], in_=ident[:, :], compare_op=ALU.not_equal,
                                         fill=1.0, base=0, pattern=[[-1, P]], channel_multiplier=1))
            nc.gpsimd.tensor_copy(ident_b[:, :], ident[:, :]).then_inc(s_ident, 1)
            for dst, value in ((neghalf, -0.5), (eps, EPS), (one, 1.0), (minus, -1.0)):
                last = nc.gpsimd.memset(dst[:, :], value)
            link(last)

            def copy(dst, src, free):
                return nc.gpsimd.tensor_tensor(dst, src, one[:, :].broadcast_to([P, free]), ALU.mult)

            def rstd_x(b):
                pool.wait_ge(x_st, (b + 1) * (2 * NT))
                nc.gpsimd.tensor_tensor(ve_x[:, b, :], mv_x[:, b, :, 1], eps[:, :],
                                        ALU.add).then_inc(x_ve, 1)
                pool.wait_ge(x_ve, b + 1)
                nc.gpsimd.tensor_tensor(rs_x[:, b, :], ve_x[:, b, :], neghalf[:, :],
                                        ALU.pow).then_inc(x_rs, 1)

            def scale_and_shift(b, stats, mv, ve, rs, nm, nb, v_sem, r_sem, m_sem, b_sem):
                pool.wait_ge(stats, (b + 1) * (2 * NT))
                nc.gpsimd.tensor_tensor(ve[:, :], mv[:, :, 1], eps[:, :], ALU.add).then_inc(v_sem, 1)
                nc.gpsimd.tensor_tensor(nm[:, :], mv[:, :, 0], minus[:, :], ALU.mult).then_inc(m_sem, 1)
                pool.wait_ge(v_sem, b + 1)
                nc.gpsimd.tensor_tensor(rs[:, :], ve[:, :], neghalf[:, :], ALU.pow).then_inc(r_sem, 1)
                pool.wait_ge(m_sem, b + 1)
                pool.wait_ge(r_sem, b + 1)
                nc.gpsimd.tensor_tensor(nb[:, :], nm[:, :], rs[:, :], ALU.mult).then_inc(b_sem, 1)

            def split_qk(b):
                for full, rest, parts, taken, r1, p2 in ((qf, qr, qp, q_tak, q_r1, q_p2),
                                                         (kf, kr, kp, k_tak, k_r1, k_p2)):
                    pool.wait_ge(taken, b * 2 + 2)
                    pool.wait_ge(p2, b)
                    nc.gpsimd.tensor_tensor(rest[:, :], full[:, :], parts[:, b % 2, 0, :],
                                            ALU.subtract).then_inc(r1, 1)
                for rest, parts, p1, p2 in ((qr, qp, q_p1, q_p2), (kr, kp, k_p1, k_p2)):
                    pool.wait_ge(p1, b + 1)
                    nc.gpsimd.tensor_tensor(parts[:, b % 2, 2, :], rest[:, :], parts[:, b % 2, 1, :],
                                            ALU.subtract).then_inc(p2, 1)

            def v_group(b, g, first):
                if not first:
                    pool.wait_ge(pv_done, b * BLK + (NT * (g + 1) - BLK))
                v = v_st[:, ds(b, 1), :].rearrange("p a (t h d) -> p (a t) h d", t=NT, h=H)
                nc.gpsimd.tensor_tensor(Vg[:, g, :, :, 0:D], v[:, :, GH * g:GH * (g + 1), :],
                                        one[:, :].unsqueeze(2).unsqueeze(3).broadcast_to([P, NT, GH, D]),
                                        ALU.mult).then_inc(vg_rdy, 1)

            pads = [0]

            def pad(ap, value):
                pads[0] += 1
                nc.gpsimd.memset(ap.rearrange("p h n -> p (h n)").bitcast(u32), value)\
                    .then_inc(s_padp, 1)
                pool.wait_ge(s_padp, pads[0])

            def split_maxima(n, g):
                pool.wait_ge(a_max, (n + 1) * (2 * NT))
                if later(n):
                    pool.wait_ge(m_rdy, n)
                m, r = mx[:, g % 2, :], mr[:, g % 2, :]
                copy(mm[:, 0:MC], m, MC).then_inc(m_p0, 1)
                pool.wait_ge(m_p0, n + 1)
                nc.gpsimd.tensor_tensor(r, m, mm[:, 0:MC], ALU.subtract).then_inc(m_r1, 1)
                pool.wait_ge(m_r1, n + 1)
                copy(mm[:, MC:2 * MC], r, MC).then_inc(m_p1, 1)
                pool.wait_ge(m_p1, n + 1)
                nc.gpsimd.tensor_tensor(mm[:, 2 * MC:3 * MC], r, mm[:, MC:2 * MC], ALU.subtract).then_inc(m_p2, 1)

            for g in range(2):
                pad(QS[g][64:KMAX, :, :], 0)
            rstd_x(0)
            link(nc.gpsimd.memset(mm[:, :], 0.0))
            for g in range(2, NG):
                pad(QS[g][64:KMAX, :, :], 0)
                pad(KS[g][64:KMAX, :, :], 0)
                pad(KS[g][KMAX:KEXP, :, :], MINUS_ONES)
            link(nc.gpsimd.memset(ones_row[:, :], 1.0))
            link(nc.gpsimd.memset(Vg[:, :, :, :, :].rearrange("p g t h c -> p (g t h c)"), 0.0))
            link(nc.gpsimd.memset(Vg[:, :, :, :, D:D + 1], 1.0))
            link(nc.gpsimd.memset(xs[:, 0:1], 0.0))
            for b in range(1, NB):
                rstd_x(b)
            split_qk(1)
            pool.wait_ge(v_tak, 1)
            for g in range(NG):
                v_group(0, g, True)
            split_qk(2)
            split_qk(3)
            split_maxima(0, 0)

            def batch(b, first, last):
                if not first:
                    v_group(b, NG - 1, False)
                split_maxima(b * NG + 1, 1)
                if not first:
                    scale_and_shift(b - 1, y_st, mv_y, ve_y, rs_y, nm_y, nb_y, y_ve, y_rs, y_nm, y_nb)
                split_maxima(b * NG + 2, 2)
                if not first:
                    add_x(b - 1)
                if not last:
                    v_group(b + 1, 0, False)
                if not first:
                    scale_and_shift(b - 1, x1_st, mv_1, ve_1, rs_1, nm_1, nb_1, x1_ve, x1_rs, x1_nm,
                                    x1_nb)
                    subtract_previous(b - 1)
                if not last:
                    v_group(b + 1, 1, False)
                split_maxima(b * NG + 3, 3)
                if not first:
                    square(b - 1)
                if not last:
                    v_group(b + 1, 2, False)
                    split_maxima(b * NG + 4, 0)
                if not first:
                    finish(b - 1)

            def add_x(e):
                pool.wait_ge(y_z, e + 1)
                nc.gpsimd.tensor_tensor(x1[:, :, :].rearrange("p t c -> p (t c)"),
                                        x_all[:, ds(e, 1), :].rearrange("p a n -> p (a n)"),
                                        zy[:, :, :].rearrange("p t c -> p (t c)"),
                                        ALU.add).then_inc(x1_rdy, 1)

            def subtract_previous(e):
                pool.wait_ge(x1T_tak, e + 1)
                nc.gpsimd.tensor_tensor(dx[:, :], xs[:, 1:1 + T], xs[:, 0:T],
                                        ALU.subtract).then_inc(d_rdy, 1)

            def square(e):
                pool.wait_ge(kf_tak, e + 1)
                nc.gpsimd.tensor_tensor(kact[:, :], krelu[:, :], krelu[:, :],
                                        ALU.mult).then_inc(ka_rdy, 1)

            def finish(e):
                scale_and_shift(e, f_st, mv_f, ve_f, rs_f, nm_f, nb_f, f_ve, f_rs, f_nm, f_nb)
                pool.wait_ge(f_z, e + 1)
                if later(e):
                    pool.wait_ge(out_wr, e * 16)
                nc.gpsimd.tensor_tensor(out_sb[:, :, :], x1[:, :, :], zf[:, :, :],
                                        ALU.add).then_inc(out_rdy, 1)

            batch(0, True, False)
            with pool.Fori(1, NB - 1) as i:
                batch(i, False, False)
            batch(NB - 1, False, True)
            e = NB - 1
            scale_and_shift(e, y_st, mv_y, ve_y, rs_y, nm_y, nb_y, y_ve, y_rs, y_nm, y_nb)
            add_x(e)
            scale_and_shift(e, x1_st, mv_1, ve_1, rs_1, nm_1, nb_1, x1_ve, x1_rs, x1_nm, x1_nb)
            subtract_previous(e)
            square(e)
            finish(e)

        @block.scalar
        def _(act):
            for i, w in ((WO, Wo), (WR, W_r), (WKF, W_k), (WVF, W_v)):
                act.dma_start(w_in[:, i, :], w[:, :]).then_inc(s_w[i], 16)
            act.wait_ge(s_wt, 5)
            nc.scalar.copy(w_T[:, 0:4, :].rearrange("p a n -> p (a n)"), psA[:, 0, 0, :])\
                .then_inc(s_wtc, 1)
            nc.scalar.copy(w_T[:, 4, :], psA[:, 0, 1, 0:E]).then_inc(s_wtc, 1)

            def take_xT(b):
                act.wait_ge(xT_rdy, b + 1)
                if b >= 2:
                    act.wait_ge(v_rdy, b - 1)
                nc.scalar.copy(xhT[:, b % 2, :], psB[:, 0, :]).then_inc(xT_tak, 1)

            def take_parts(b, ps, full, parts, bias, ready, r1, taken):
                act.wait_ge(ready, b + 1)
                if b >= 1:
                    act.wait_ge(r1, b)
                if b >= 2:
                    act.wait_ge(qk_wr[b - 2], 16 * WW)
                nc.scalar.activation(full[:, :], ps[:, :], ACT.Identity, bias=bias).then_inc(taken, 1)
                nc.scalar.activation(parts[:, b % 2, 0, :], ps[:, :], ACT.Identity,
                                     bias=bias).then_inc(taken, 1)

            def take_q(b):
                take_parts(b, psO, qf, qp, vec[:, V_BQ:V_BQ + 1], q_rdy, q_r1, q_tak)

            def take_k(b):
                take_parts(b, psM, kf, kp, b_kl[:, 0:1], k_rdy, k_r1, k_tak)

            def second_part(b, rest, parts, r1, p1):
                act.wait_ge(r1, b + 1)
                nc.scalar.copy(parts[:, b % 2, 1, :], rest[:, :]).then_inc(p1, 1)

            def take_v(b):
                act.wait_ge(v_rdy, b + 1)
                nc.scalar.copy(v_st[:, b, :], psB[:, 1, :]).then_inc(v_tak, 1)

            take_xT(0)
            act.wait_ge(s_wkl, 2)
            nc.scalar.copy(w_kl[:, :, :].rearrange("p a n -> p (a n)"), psA[:, 1, 0, 0:2 * E])\
                .then_inc(s_wklc, 1)
            act.wait_ge(s_vec, 16 * 7)
            take_q(0)
            act.wait_ge(s_bklc, 2)
            take_k(0)
            take_v(0)
            for b in range(1, NB):
                take_xT(b)
                take_q(b)
                take_k(b)
                second_part(b, qr, qp, q_r1, q_p1)
                take_v(b)
                second_part(b, kr, kp, k_r1, k_p1)

            def take_maxima(n):
                act.wait_ge(m_rdy, n + 1)
                if later(n):
                    act.wait_ge(m_in, n * 16)
                nc.scalar.copy(mmT[:, :], psM_b[0:PARTS * MC, 0:P]).then_inc(m_tak, 1)

            def take_o(n):
                act.wait_ge(pv_done, (n + 1) * NT)
                if later(n):
                    act.wait_ge(on_rdy, n)
                nc.scalar.copy(o_sb[:, :], psO[:, :]).then_inc(o_tak, 1)

            def take_oT(e):
                act.wait_ge(oT_rdy, e + 1)
                nc.scalar.copy(oT[:, :], psM[:, :]).then_inc(oT_tak, 1)

            def take_x1T(e):
                act.wait_ge(x1T_rdy, e + 1)
                nc.scalar.copy(xs[:, 1:1 + T], psM[:, :]).then_inc(x1T_tak, 1)

            def take_kf(e):
                act.wait_ge(kf_rdy, e + 1)
                nc.scalar.activation(krelu[:, :], psM[:, :], ACT.Relu).then_inc(kf_tak, 1)

            def take_r(e):
                act.wait_ge(r_rdy, e + 1)
                nc.scalar.activation(er[:, :], psM[:, :], ACT.Exp, scale=-1.0).then_inc(r_tak, 1)

            take_maxima(0)

            def normalise_rows(e, src, dst, rs, nb, shifts, done, before):
                act.wait_ge(shifts, e + 1)
                if before is not None and later(e):
                    act.wait_ge(before, e)
                for t in range(NT):
                    last = nc.scalar.activation(dst[:, t, :], src[:, t, :], ACT.Identity,
                                                scale=rs[:, t:t + 1], bias=nb[:, t:t + 1])
                last.then_inc(done, 1)

            def normalise_y(e):
                normalise_rows(e, ysb, zy, rs_y, nb_y, y_nb, y_z, x1_rdy)

            def normalise_x1(e):
                normalise_rows(e, x1, x1h, rs_1, nb_1, x1_nb, x1_h, None)

            def normalise_f(e):
                normalise_rows(e, f_sb, zf, rs_f, nb_f, f_nb, f_z, out_rdy)

            def exponentials(b, n, i, last):
                act.wait_ge(b_rdy, b * (BLK * GH) + (n * GH + i + 1))
                if n >= 2 or later(b):
                    act.wait_ge(pv_done, b * BLK + (n - 1))
                nc.scalar.activation(pT[:, n % 2, i, :], score_bank(n, i, last), ACT.Exp,
                                     scale=SCALE).then_inc(e_rdy, 1)

            def batch(b, first, last):
                for n in range(BLK):
                    if n % NT == 1 and (n > 1 or not first):
                        take_o(b * NG + (n // NT - 1))
                    if n % NT == 3 and (n < 15 or not last):
                        take_maxima(b * NG + (n // NT + 1))
                    if n == 6 and not first:
                        normalise_y(b - 1)
                    if n == 8 and not first:
                        normalise_x1(b - 1)
                    if n == 9 and not first:
                        take_x1T(b - 1)
                    if n == 12 and not first:
                        take_r(b - 1)
                    exponentials(b, n, 0, last)
                    exponentials(b, n, 1, last)
                    if n == 3 and not first:
                        take_oT(b - 1)
                    if n == 11 and not first:
                        take_kf(b - 1)
                    exponentials(b, n, 2, last)
                    exponentials(b, n, 3, last)
                if not first:
                    normalise_f(b - 1)

            batch(0, True, False)
            with act.Fori(1, NB - 1) as i:
                batch(i, False, False)
            batch(NB - 1, False, True)
            take_o(NB * NG - 1)
            take_oT(NB - 1)
            normalise_y(NB - 1)
            normalise_x1(NB - 1)
            take_x1T(NB - 1)
            take_kf(NB - 1)
            take_r(NB - 1)
            normalise_f(NB - 1)

        @block.vector
        def _(dve):
            def stats(src, st, mv, s):
                for t in range(NT):
                    nc.vector.bn_stats(st[:, t, :], src(t)).then_inc(s[0], 1)
                dve.wait_ge(s[0], s[1] * (2 * NT) + NT)
                nc.vector.memset(idle[:, :], 0.0)
                for t in range(NT):
                    nc.vector.bn_aggr(mv[:, t, :], st[:, t, :]).then_inc(s[0], 1)

            def x_stats(b):
                dve.wait_ge(s_xin[b], 16)
                stats(lambda t: x_all[:, b, E * t:E * (t + 1)], st_x[:, b, :, :], mv_x[:, b, :, :], (x_st, b))

            def x_normalise(b):
                dve.wait_ge(x_rs, b + 1)
                for t in range(NT):
                    last = nc.vector.tensor_scalar(xh[:, b, t, :], x_all[:, b, E * t:E * (t + 1)],
                                                   mv_x[:, b, t, 0:1], rs_x[:, b, t:t + 1],
                                                   ALU.subtract, ALU.mult)
                last.then_inc(x_h, 1)

            def split_first(full, rest, parts, taken, r1, p1, p2):
                dve.wait_ge(taken, 2)
                nc.vector.tensor_tensor(rest[:, :], full[:, :], parts[:, 0, 0, :],
                                        ALU.subtract).then_inc(r1, 1)
                dve.wait_ge(r1, 1)
                nc.vector.tensor_copy(parts[:, 0, 1, :], rest[:, :]).then_inc(p1, 1)
                dve.wait_ge(p1, 1)
                nc.vector.tensor_tensor(parts[:, 0, 2, :], rest[:, :], parts[:, 0, 1, :],
                                        ALU.subtract).then_inc(p2, 1)

            def pad(ap, value):
                nc.vector.memset(ap.rearrange("p h n -> p (h n)").bitcast(u32), value)\
                    .then_inc(s_padv, 1)

            x_stats(0)
            x_normalise(0)
            pad(KS[0][64:KMAX, :, :], 0)
            pad(KS[0][KMAX:KEXP, :, :], MINUS_ONES)
            dve.wait_ge(s_vec, 16 * 7)
            dve.wait_ge(s_bkl, 2)
            nc.vector.tensor_tensor(b_kl[:, 0:1], psA[:, 1, 1, 0:1], vec[:, V_BL:V_BL + 1],
                                    ALU.add).then_inc(s_bklc, 1)
            nc.vector.tensor_tensor(b_kl[:, 1:2], psA[:, 1, 1, 1:2], vec[:, V_BL:V_BL + 1],
                                    ALU.add).then_inc(s_bklc, 1)
            split_first(qf, qr, qp, q_tak, q_r1, q_p1, q_p2)
            dve.wait_ge(s_bklc, 2)
            nc.vector.tensor_copy(bvl_wide[:, :], b_kl[:, 1:2].broadcast_to([P, P])).then_inc(s_wide, 1)
            split_first(kf, kr, kp, k_tak, k_r1, k_p1, k_p2)
            x_stats(1)
            x_stats(2)
            x_normalise(1)
            pad(KS[1][64:KMAX, :, :], 0)
            pad(KS[1][KMAX:KEXP, :, :], MINUS_ONES)
            x_stats(3)
            x_normalise(2)
            x_normalise(3)
            dve.wait_ge(s_bo, 1)
            for t in range(NT):
                last = nc.vector.tensor_copy(bout[:, t, :], psA[:, 1, 1, 0:E])
            last.then_inc(s_boc, 1)

            def maxima(group, a, g, h, u, free):
                dve.wait_ge(a_rdy, a * 2 + (u + 1))
                if h == 0 and u == 0 and free:
                    dve.wait_ge(m_p2, group - 1)
                c = NT * h + 2 * u
                nc.vector.tensor_reduce(out=mx[:, g % 2, c:c + 2], in_=psA[:, u, :, :],
                                        axis=AX.X, op=ALU.max).then_inc(a_max, 1)

            def normalise(b, g, wait_oq):
                n = b * NG + g
                dve.wait_ge(on_rdy, n + 1)
                o = psM[:, :].rearrange("p (t h c) -> p t h c", t=NT, h=GH)
                nc.vector.reciprocal(rsum[:, :, :], o[:, :, :, D]).then_inc(o_rec, 1)
                dve.wait_ge(o_rec, n + 1)
                if wait_oq:
                    dve.wait_ge(oT_rdy, b)
                nc.vector.tensor_tensor(oq[:, :, GH * g:GH * (g + 1), :], o[:, :, :, 0:D],
                                        rsum[:, :, :].unsqueeze(3).broadcast_to([P, NT, GH, D]),
                                        ALU.mult).then_inc(on_tak, 1)

            for a in range(LEAD):
                for u in range(2):
                    maxima(a // GH, a, a // GH, a % GH, u, False)

            def take_y(e):
                dve.wait_ge(y_rdy, e + 1)
                nc.vector.tensor_tensor(ysb[:, :, :].rearrange("p t c -> p (t c)"), psM[:, :],
                                        bout[:, :, :].rearrange("p t c -> p (t c)"),
                                        ALU.add).then_inc(y_tak, 1)
                dve.wait_ge(y_tak, e + 1)

            def y_stats(e):
                stats(lambda t: ysb[:, t, :], st_y, mv_y, (y_st, e))

            def x1_stats(e):
                dve.wait_ge(x1_rdy, e + 1)
                stats(lambda t: x1[:, t, :], st_1, mv_1, (x1_st, e))

            def mix(e, dst, mu, s):
                dve.wait_ge(d_rdy, e + 1)
                nc.vector.scalar_tensor_tensor(out=dst[:, :], in0=dx[:, :], scalar=vec[:, mu:mu + 1],
                                               in1=xs[:, 0:T], op0=ALU.mult, op1=ALU.add).then_inc(s, 1)

            def sigmoid_sum(e):
                dve.wait_ge(r_tak, e + 1)
                nc.vector.tensor_scalar(rr[:, :], er[:, :], 1.0, None, ALU.add).then_inc(r_add, 1)
                dve.wait_ge(r_add, e + 1)

            def take_f(e):
                dve.wait_ge(f_rdy, e + 1)
                dve.wait_ge(r_rec, (e + 1) * NT)
                nc.vector.tensor_tensor(f_sb[:, :, :].rearrange("p t c -> p (t c)"), psM[:, :],
                                        er[:, :], ALU.mult).then_inc(f_tak, 1)
                dve.wait_ge(f_tak, e + 1)

            def f_stats(e):
                stats(lambda t: f_sb[:, t, :], st_f, mv_f, (f_st, e))

            def sigmoid_part(e, t):
                nc.vector.reciprocal(er[:, E * t:E * (t + 1)], rr[:, E * t:E * (t + 1)])\
                    .then_inc(r_rec, 1)

            def batch(b, first, last):
                for n in range(BLK):
                    ahead = n + LEAD
                    g, h = ahead // GH % NG, ahead % GH
                    if n == 2 and not first:
                        normalise(b - 1, NG - 1, False)
                    if n == 4 and not first:
                        take_y(b - 1)
                    if n in (6, 10):
                        normalise(b, n // NT - 1, n == 6 and not first)
                    if n == 14:
                        if not first:
                            take_f(b - 1)
                        normalise(b, 2, False)
                    if ahead < BLK or not last:
                        maxima(b * NG + ahead // GH, b * BLK + ahead, g, h, 0, ahead >= 2 * GH or not first)
                    if n == 12 and not first:
                        sigmoid_sum(b - 1)
                        sigmoid_part(b - 1, 0)
                    if n == 13 and not first:
                        sigmoid_part(b - 1, 2)
                    if ahead < BLK or not last:
                        maxima(b * NG + ahead // GH, b * BLK + ahead, g, h, 1, False)
                    if n == 4 and not first:
                        y_stats(b - 1)
                    if n == 6 and not first:
                        x1_stats(b - 1)
                    if n == 10 and not first:
                        mix(b - 1, xk, V_MK, xk_rdy)
                        mix(b - 1, xr, V_MR, xr_rdy)
                    if n == 12 and not first:
                        sigmoid_part(b - 1, 1)
                    if n == 13 and not first:
                        sigmoid_part(b - 1, 3)
                    if n == 14 and not first:
                        f_stats(b - 1)

            batch(0, True, False)
            with dve.Fori(1, NB - 1) as i:
                batch(i, False, False)
            batch(NB - 1, False, True)
            e = NB - 1
            normalise(e, NG - 1, False)
            take_y(e)
            y_stats(e)
            x1_stats(e)
            mix(e, xk, V_MK, xk_rdy)
            mix(e, xr, V_MR, xr_rdy)
            sigmoid_sum(e)
            for t in range(NT):
                sigmoid_part(e, t)
            take_f(e)
            f_stats(e)

        @block.tensor
        def _(pe):
            pe.wait_ge(s_ident, 1)
            for j, i in ((T_WK, WK), (T_WV, WV), (T_WR, WR), (T_WKF, WKF), (T_WVF, WVF)):
                pe.wait_ge(s_w[i], 16)
                nc.tensor.transpose(psA[:, 0, j // 4, E * (j % 4):E * (j % 4 + 1)], w_in[:, i, :],
                                    ident[:, :]).then_inc(s_wt, 1)

            def product_by_tile(lhs, rhs, ready):
                for t in range(NT):
                    last = nc.tensor.matmul(psM[:, E * t:E * (t + 1)], lhs[:, P * t:P * (t + 1)], rhs,
                                            start=True, stop=True)
                last.then_inc(ready, 1)

            def transposes(src, ready):
                for t in range(NT):
                    last = nc.tensor.transpose(psM[:, P * t:P * (t + 1)], src(t), ident[:, :])
                last.then_inc(ready, 1)

            def job_xT(e):
                pe.wait_ge(x_h, e + 1)
                for t in range(NT):
                    last = nc.tensor.transpose(psB[:, 0, P * t:P * (t + 1)], xh[:, e, t, :], ident[:, :])
                last.then_inc(xT_rdy, 1)

            def job_q(e):
                pe.wait_ge(xT_tak, e + 1)
                if e:
                    pe.wait_ge(q_tak, 2 * e)
                nc.tensor.matmul(psO[:, :], w_in[:, WQ, :], xhT[:, e % 2, :], start=True, stop=True)\
                    .then_inc(q_rdy, 1)

            def job_k(e):
                if e:
                    pe.wait_ge(k_tak, 2 * e)
                nc.tensor.matmul(psM[:, :], w_kl[:, 0, :], xhT[:, e % 2, :], start=True, stop=True)\
                    .then_inc(k_rdy, 1)

            def job_v(e):
                if e:
                    pe.wait_ge(v_tak, e)
                for t in range(NT):
                    last = nc.tensor.matmul(psB[:, 1, E * t:E * (t + 1)], xhT[:, e % 2, P * t:P * (t + 1)],
                                            w_kl[:, 1, :], start=True, stop=True)
                last.then_inc(v_rdy, 1)

            def job_m(n):
                pe.wait_ge(m_p2, n + 1)
                nc.tensor.transpose(psM_b[:, 0:P], mm[:, :], ident_b[:, :]).then_inc(m_rdy, 1)

            def job_on(n):
                pe.wait_ge(o_tak, n + 1)
                transposes(lambda t: o_sb[:, P * t:P * (t + 1)], on_rdy)

            def job_oT(e):
                pe.wait_ge(on_tak, (e + 1) * NG)
                transposes(lambda t: oq[:, t, :, :].rearrange("p h d -> p (h d)"), oT_rdy)

            def job_y(e):
                pe.wait_ge(oT_tak, e + 1)
                product_by_tile(oT, w_in[:, WO, :], y_rdy)

            def job_x1T(e):
                pe.wait_ge(x1_h, e + 1)
                transposes(lambda t: x1h[:, t, :], x1T_rdy)

            def job_kf(e):
                pe.wait_ge(xk_rdy, e + 1)
                nc.tensor.matmul(psM[:, :], w_T[:, T_WKF, :], xk[:, :], start=True, stop=True)\
                    .then_inc(kf_rdy, 1)

            def job_r(e):
                pe.wait_ge(xr_rdy, e + 1)
                product_by_tile(xr, w_T[:, T_WR, :], r_rdy)

            def job_f(e):
                pe.wait_ge(ka_rdy, e + 1)
                product_by_tile(kact, w_T[:, T_WVF, :], f_rdy)

            def scores_for_maxima(e, a, g, h, u, later_pair):
                if u == 0:
                    if h == 0:
                        pe.wait_ge(ld[g], (e + 1) * (16 * LW))
                if later_pair:
                    pe.wait_ge(a_max, a * 2 + (u - 1))
                for j in range(2):
                    t = 2 * u + j
                    last = nc.tensor.matmul(psA[:, u, j, :], QS[g][0:KMAX, h, P * t:P * (t + 1)],
                                            KS[g][0:KMAX, h, :], start=True, stop=True)
                last.then_inc(a_rdy, 1)

            def scores_for_exponentials(b, n, i, later_tile, last):
                g, t = n // NT, n % NT
                if t == 0 and i == 0:
                    pe.wait_ge(m_in, b * (16 * NG) + 16 * (g + 1))
                if last and n >= TAIL and i >= 2 and n == TAIL:
                    if i == 2:
                        pe.wait_ge(a_max, 2 * BLK * NB)
                elif last and (n > TAIL or n == TAIL and i >= 2):
                    pe.wait_ge(e_rdy, b * (BLK * GH) + (n * GH + i - 3))
                elif later_tile:
                    pe.wait_ge(e_rdy, b * (BLK * GH) + (n * GH + i - 1))
                nc.tensor.matmul(score_bank(n, i, last), KS[g][0:KEXP, i, P * t:P * (t + 1)],
                                 QS[g][0:KEXP, i, :], start=True, stop=True).then_inc(b_rdy, 1)

            def times_v(b, n, later_group):
                g, t = n // NT % NG, n % NT
                if t == 0:
                    pe.wait_ge(vg_rdy, b * NG + (n // NT + 1))
                    if later_group:
                        pe.wait_ge(o_tak, b * NG + n // NT)
                pe.wait_ge(e_rdy, b * (BLK * GH) + GH * (n + 1))
                for i in range(GH):
                    last = nc.tensor.matmul(psO[QUAD * i:QUAD * (i + 1), :], Vg[:, g, t, i, :],
                                            pT[:, n % 2, i, :], start=(t == 0), stop=(t == NT - 1))
                last.then_inc(pv_done, 1)

            job_xT(0)
            pe.wait_ge(s_wtc, 2)
            pe.wait_ge(s_w[WL], 16)
            for j in range(2):
                nc.tensor.matmul(psA[:, 1, 0, E * j:E * (j + 1)], w_T[:, T_WK + j, :], w_in[:, WL, :],
                                 start=True, stop=True).then_inc(s_wkl, 1)
            pe.wait_ge(s_vec, 16 * 7)
            for j in range(2):
                nc.tensor.matmul(psA[:, 1, 1, j:j + 1], w_in[:, WL, :], vec[:, V_BK + j:V_BK + j + 1],
                                 start=True, stop=True).then_inc(s_bkl, 1)
            job_q(0)
            pe.wait_ge(s_wklc, 1)
            job_k(0)
            job_v(0)
            pe.wait_ge(s_wide, 1)
            pe.wait_ge(s_w[WO], 16)
            pe.wait_ge(s_const, 5)
            nc.tensor.matmul(psA[:, 1, 1, 0:E], bvl_wide[:, :], w_in[:, WO, :], start=True, stop=False)
            nc.tensor.matmul(psA[:, 1, 1, 0:E], ones_row[:, :], bo_row[:, :], start=False,
                             stop=True).then_inc(s_bo, 1)
            job_xT(1)
            job_q(1)
            job_k(1)
            job_v(1)
            for a in range(LEAD):
                for u in range(2):
                    if a == 0 and u == 1:
                        pe.wait_ge(s_boc, 1)
                    scores_for_maxima(0, a, a // GH, a % GH, u, a > 0)
                if a in (0, 2):
                    job_xT(a // 2 + 2)
                if a in (1, 3):
                    job_q(a // 2 + 2)
                    job_k(a // 2 + 2)
                if a in (2, 4):
                    job_v(a // 2 + 1)
            pe.wait_ge(k_tak, 2 * NB)
            job_m(0)
            pe.wait_ge(v_tak, NB)
            pe.wait_ge(q_tak, 2 * NB)

            def batch(b, first, last):
                def job(name, do):
                    pe.wait_ge(*job_before(b, name, first, last))
                    do()

                for n in range(BLK):
                    scores_for_exponentials(b, n, 0, n > 0 or not first, last)
                    scores_for_exponentials(b, n, 1, n > 0 or not first, last)
                    if n == 3 and not first:
                        job("oT", lambda: job_oT(b - 1))
                    if n == 11 and not first:
                        job("kf", lambda: job_kf(b - 1))
                    if n == 14:
                        job("on2", lambda: job_on(b * NG + 2))
                    ahead = n + LEAD
                    if ahead < BLK or not last:
                        for u in range(2):
                            scores_for_maxima(b + ahead // BLK, b * BLK + ahead, ahead // GH % NG,
                                              ahead % GH, u, True)
                    scores_for_exponentials(b, n, 2, True, last)
                    scores_for_exponentials(b, n, 3, True, last)
                    if n or not first:
                        times_v_before(b, n, first)
                    if n == 1 and not first:
                        job("on-1", lambda: job_on(b * NG - 1))
                    if n in (2, 6, 10):
                        job(f"m{n // NT + 1}", lambda: job_m(b * NG + (n // NT + 1)))
                    if n == 3 and not first:
                        job("y", lambda: job_y(b - 1))
                    if n in (5, 9):
                        job(f"on{n // NT - 1}", lambda: job_on(b * NG + (n // NT - 1)))
                    if n == 8 and not first:
                        job("x1T", lambda: job_x1T(b - 1))
                    if n == 11 and not first:
                        job("r", lambda: job_r(b - 1))
                    if n == 13 and not first:
                        job("f", lambda: job_f(b - 1))
                    if n == 14 and not last:
                        job("m4", lambda: job_m(b * NG + NG))

            def times_v_before(b, n, first):
                if n:
                    times_v(b, n - 1, n > 1 or not first)
                else:
                    times_v(b - 1, BLK - 1, True)

            batch(0, True, False)
            with pe.Fori(1, NB - 1) as i:
                batch(i, False, False)
            batch(NB - 1, False, True)
            e = NB - 1
            times_v(e, BLK - 1, True)
            pe.wait_ge(on_tak, NG * e + 3)
            job_on(NG * e + 3)
            job_oT(e)
            job_y(e)
            pe.wait_ge(y_tak, e + 1)
            job_x1T(e)
            job_kf(e)
            pe.wait_ge(kf_tak, e + 1)
            job_r(e)
            pe.wait_ge(r_tak, e + 1)
            job_f(e)


_INS = ["x", "Wq", "bq", "Wk", "bk", "Wv", "bv", "Wl", "bl", "Wo", "bo"]
_FFN = ["W_r", "W_k", "W_v", "mu_r", "mu_k"]


def kernel(**inputs):
    import numpy as _np
    import concourse.bacc as _bacc
    from concourse import mybir as _mybir
    from concourse.bass_utils import run_bass_kernel_spmd as _run

    nc = _bacc.Bacc("TRN2", target_bir_lowering=False, num_devices=1)
    arrays, args = {}, []
    for name in ["L0_attn_" + n for n in _INS] + ["L0_ffn_" + n for n in _FFN]:
        a = _np.ascontiguousarray(inputs[name])
        arrays[f"in_{name}_dram"] = a
        args.append(nc.dram_tensor(f"in_{name}_dram", a.shape, _mybir.dt.from_np(a.dtype),
                                   kind="ExternalInput").ap())
    shape = inputs["L0_attn_x"].shape
    args.append(nc.dram_tensor("out_dram", shape, _mybir.dt.float32, kind="ExternalOutput").ap())
    sandwich_kernel(nc, *args)
    r = _run(nc, [arrays], core_ids=[0])
    return r.results[0]["out_dram"]
```

```python
import concourse.bass as bass
from concourse import mybir
from contextlib import ExitStack


def sandwich_kernel(nc, x, Wq, bq, Wk, bk, Wv, bv, Wl, bl, Wo, bo, W_r, W_k, W_v, mu_r, mu_k, out):
    fp32 = mybir.dt.float32
    bf16 = mybir.dt.bfloat16
    u32 = mybir.dt.uint32
    ALU = mybir.AluOpType
    ACT = mybir.ActivationFunctionType
    AX = mybir.AxisListType
    ds = bass.ds

    NB, T, E = x.shape
    H = 16
    D = E // H
    P = 128
    NT = T // P
    GH = 4
    NG = H // GH
    BLK = NG * NT
    LEAD = 6
    PARTS = 3
    ROWS = PARTS * PARTS * D
    KMAX = 96
    KEXP = KMAX + PARTS
    QUAD = 32
    SCALE = float(D) ** -0.5
    EPS = 1e-5
    MINUS_ONES = 0xBF80BF80

    ctx = ExitStack()
    with ctx:
        def sb(name, shape, dt=fp32):
            return ctx.enter_context(nc.sbuf_tensor(name, shape, dt))

        def pb(name, shape, dt=fp32):
            return ctx.enter_context(nc.psum_tensor(name, shape, dt))

        def sem(name):
            return ctx.enter_context(nc.semaphore(name))

        q_scr = nc.dram_tensor("q_scr", [NB, PARTS, D, H, T], bf16, kind="Internal").ap()
        k_scr = nc.dram_tensor("k_scr", [NB, PARTS, D, H, T], bf16, kind="Internal").ap()

        ident = sb("ident", [P, P])
        ident_b = sb("ident_b", [P, P], bf16)
        w_in = sb("w_in", [P, 9, E])
        WQ, WK, WV, WL, WO, WR, WKF, WVF = range(8)
        w_T = sb("w_T", [P, 5, E])
        T_WK, T_WV, T_WR, T_WKF, T_WVF = range(5)
        w_kl = sb("w_kl", [P, 2, E])
        vec = sb("vec", [P, 8])
        V_BQ, V_BK, V_BV, V_BL, V_MR, V_MK = range(6)
        b_kl = sb("b_kl", [P, 2])
        bvl_wide = sb("bvl_wide", [P, P])
        bo_row = sb("bo_row", [1, E])
        ones_row = sb("ones_row", [1, P])
        bout = sb("bout", [P, NT, E])
        neghalf = sb("neghalf", [P, NT])
        eps = sb("eps", [P, NT])
        one = sb("one", [P, 1])
        minus = sb("minus", [P, NT])
        idle = sb("idle", [P, 1])
        idle_p = sb("idle_p", [P, 1])
        warm = sb("warm", [P, T], bf16)

        x_all = sb("x_all", [P, NB, NT * E])
        st_x = sb("st_x", [P, NB, NT, 6])
        mv_x = sb("mv_x", [P, NB, NT, 2])
        ve_x = sb("ve_x", [P, NB, NT])
        rs_x = sb("rs_x", [P, NB, NT])
        xh = sb("xh", [P, NB, NT, E])
        xhT = sb("xhT", [P, 2, T])
        qf = sb("qf", [P, T])
        qr = sb("qr", [P, T])
        qp = sb("qp", [P, 2, PARTS, T], bf16)
        kf = sb("kf", [P, T])
        kr = sb("kr", [P, T])
        kp = sb("kp", [P, 2, PARTS, T], bf16)
        v_st = sb("v_st", [P, NB, NT * H * D])

        QS = [sb(f"QS{g}", [P, GH, T], bf16) for g in range(NG)]
        KS = [sb(f"KS{g}", [P, GH, T], bf16) for g in range(NG)]
        Vg = sb("Vg", [P, NG, NT, GH, QUAD])
        mx = sb("mx", [P, 2, GH * NT])
        mr = sb("mr", [P, 2, GH * NT])
        MC = GH * NT
        mm = sb("mm", [P, P], bf16)
        mmT = sb("mmT", [PARTS * MC, P], bf16)
        pT = sb("pT", [P, 2, GH, T])
        o_sb = sb("o_sb", [P, T])
        rsum = sb("rsum", [P, NT, GH])
        oq = sb("oq", [P, NT, H, D])

        oT = sb("oT", [P, T])
        ysb = sb("ysb", [P, NT, E])
        st_y = sb("st_y", [P, NT, 6])
        mv_y = sb("mv_y", [P, NT, 2])
        ve_y = sb("ve_y", [P, NT])
        rs_y = sb("rs_y", [P, NT])
        nm_y = sb("nm_y", [P, NT])
        nb_y = sb("nb_y", [P, NT])
        zy = sb("zy", [P, NT, E])
        x1 = sb("x1", [P, NT, E])
        st_1 = sb("st_1", [P, NT, 6])
        mv_1 = sb("mv_1", [P, NT, 2])
        ve_1 = sb("ve_1", [P, NT])
        rs_1 = sb("rs_1", [P, NT])
        nm_1 = sb("nm_1", [P, NT])
        nb_1 = sb("nb_1", [P, NT])
        x1h = sb("x1h", [P, NT, E])
        xs = sb("xs", [P, 1 + T])
        dx = sb("dx", [P, T])
        xr = sb("xr", [P, T])
        xk = sb("xk", [P, T])
        krelu = sb("krelu", [P, T])
        kact = sb("kact", [P, T])
        er = sb("er", [P, NT * E])
        rr = sb("rr", [P, NT * E])
        f_sb = sb("f_sb", [P, NT, E])
        st_f = sb("st_f", [P, NT, 6])
        mv_f = sb("mv_f", [P, NT, 2])
        ve_f = sb("ve_f", [P, NT])
        rs_f = sb("rs_f", [P, NT])
        nm_f = sb("nm_f", [P, NT])
        nb_f = sb("nb_f", [P, NT])
        zf = sb("zf", [P, NT, E])
        out_sb = sb("out_sb", [P, NT, E])

        w_mix = sb("w_mix", [P, 5, E])
        w_cen = sb("w_cen", [P, 2, E])
        st_w = sb("st_w", [P, 2, 6])
        mv_w = sb("mv_w", [P, 2, 2])

        psA = pb("psA", [P, 2, 2, T])
        psB = pb("psB", [P, 2, T])
        psO = pb("psO", [P, T])
        psM = pb("psM", [P, T])
        psM_b = psM[:, :].bitcast(bf16)

        s_vec = sem("s_vec")
        s_w = [sem(f"s_w{i}") for i in range(8)]
        s_xin = [sem(f"s_xin{b}") for b in range(NB)]
        s_const = sem("s_const")
        s_ident = sem("s_ident")
        s_warm = sem("s_warm")
        s_padp = sem("s_padp")
        s_padv = sem("s_padv")
        s_wt = sem("s_wt")
        s_wtc = sem("s_wtc")
        s_wkl = sem("s_wkl")
        s_wklc = sem("s_wklc")
        s_bkl = sem("s_bkl")
        s_bklc = sem("s_bklc")
        s_wide = sem("s_wide")
        s_bo = sem("s_bo")
        s_boc = sem("s_boc")

        x_st = sem("x_st")
        x_ve = sem("x_ve")
        x_rs = sem("x_rs")
        x_h = sem("x_h")
        xT_rdy = sem("xT_rdy")
        xT_tak = sem("xT_tak")
        q_rdy = sem("q_rdy")
        q_tak = sem("q_tak")
        q_r1 = sem("q_r1")
        q_p1 = sem("q_p1")
        q_p2 = sem("q_p2")
        k_rdy = sem("k_rdy")
        k_tak = sem("k_tak")
        k_r1 = sem("k_r1")
        k_p1 = sem("k_p1")
        k_p2 = sem("k_p2")
        v_rdy = sem("v_rdy")
        v_tak = sem("v_tak")
        q_wr = [sem(f"q_wr{b}") for b in range(NB)]
        k_wr = [sem(f"k_wr{b}") for b in range(NB)]
        ld = [sem(f"ld{g}") for g in range(NG)]
        LW = PARTS + 1
        vg_rdy = sem("vg_rdy")

        a_rdy = sem("a_rdy")
        a_max = sem("a_max")
        m_p0 = sem("m_p0")
        m_r1 = sem("m_r1")
        m_p1 = sem("m_p1")
        m_p2 = sem("m_p2")
        m_rdy = sem("m_rdy")
        m_tak = sem("m_tak")
        m_in = sem("m_in")
        b_rdy = sem("b_rdy")
        e_rdy = sem("e_rdy")
        pv_done = sem("pv_done")
        o_tak = sem("o_tak")
        on_rdy = sem("on_rdy")
        o_rec = sem("o_rec")
        on_tak = sem("on_tak")

        oT_rdy = sem("oT_rdy")
        oT_tak = sem("oT_tak")
        y_rdy = sem("y_rdy")
        y_tak = sem("y_tak")
        y_st = sem("y_st")
        y_ve = sem("y_ve")
        y_rs = sem("y_rs")
        y_nm = sem("y_nm")
        y_nb = sem("y_nb")
        y_z = sem("y_z")
        x1_rdy = sem("x1_rdy")
        x1_st = sem("x1_st")
        x1_ve = sem("x1_ve")
        x1_rs = sem("x1_rs")
        x1_nm = sem("x1_nm")
        x1_nb = sem("x1_nb")
        x1_h = sem("x1_h")
        x1T_rdy = sem("x1T_rdy")
        x1T_tak = sem("x1T_tak")
        d_rdy = sem("d_rdy")
        xk_rdy = sem("xk_rdy")
        xr_rdy = sem("xr_rdy")
        kf_rdy = sem("kf_rdy")
        kf_tak = sem("kf_tak")
        ka_rdy = sem("ka_rdy")
        r_rdy = sem("r_rdy")
        r_tak = sem("r_tak")
        r_add = sem("r_add")
        r_rec = sem("r_rec")
        f_rdy = sem("f_rdy")
        f_tak = sem("f_tak")
        f_st = sem("f_st")
        f_ve = sem("f_ve")
        f_rs = sem("f_rs")
        f_nm = sem("f_nm")
        f_nb = sem("f_nb")
        f_z = sem("f_z")
        out_rdy = sem("out_rdy")
        out_wr = sem("out_wr")

        HALF = NT // 2
        z_w = sem("z_w")
        z_c = sem("z_c")
        z_o = sem("z_o")
        z_on = sem("z_on")
        z_rec = sem("z_rec")
        z_oq = sem("z_oq")
        z_oT = sem("z_oT")
        z_oTc = sem("z_oTc")
        z_yp = sem("z_yp")
        z_yst = sem("z_yst")
        z_yve = sem("z_yve")
        z_yrs = sem("z_yrs")
        z_x1 = sem("z_x1")
        z_1st = sem("z_1st")
        z_1ve = sem("z_1ve")
        z_1rs = sem("z_1rs")
        z_1h = sem("z_1h")
        z_xT = sem("z_xT")
        z_xs = sem("z_xs")
        z_r = sem("z_r")
        z_kf = sem("z_kf")
        z_er = sem("z_er")
        z_add = sem("z_add")
        z_relu = sem("z_relu")
        z_ka = sem("z_ka")
        z_gate = sem("z_gate")
        z_fp = sem("z_fp")
        z_f = sem("z_f")
        z_fst = sem("z_fst")
        z_fve = sem("z_fve")
        z_frs = sem("z_frs")
        z_fc = sem("z_fc")
        z_out = sem("z_out")
        z_wr = sem("z_wr")
        z_bank = {"on": (psA[:, 0, 0, :], psA[:, 0, 1, :]), "oT": (psA[:, 1, 0, :], psA[:, 1, 1, :]),
                  "y": (psB[:, 0, :], psB[:, 1, :]), "x1T": (psM[:, :], psO[:, :])}
        z_bank.update({"r": z_bank["on"], "kf": z_bank["oT"], "f": z_bank["y"]})

        def z_cols(u):
            return slice(HALF * P * u, HALF * P * (u + 1))

        def z_tiles(u):
            return range(HALF * u, HALF * (u + 1))

        JOBS = [("F", "on-1", on_tak, NG, 0), ("M", "m1", m_tak, NG, 2), ("F", "oT", oT_tak, 1, 0),
                ("F", "y", y_tak, 1, 0), ("N", "on0", on_tak, NG, 1), ("M", "m2", m_tak, NG, 3),
                ("F", "x1T", x1T_tak, 1, 0), ("N", "on1", on_tak, NG, 2), ("M", "m3", m_tak, NG, 4),
                ("F", "r", r_tak, 1, 0), ("F", "kf", kf_tak, 1, 0), ("F", "f", f_tak, 1, 0),
                ("L", "m4", m_tak, NG, 5), ("N", "on2", on_tak, NG, 3)]
        PE_AT = {"on-1": (2, 1), "m1": (2, 4), "oT": (3, 0), "y": (3, 3), "on0": (5, 1), "m2": (6, 2),
                 "x1T": (8, 4), "on1": (9, 1), "m3": (10, 3), "r": (10, 4), "kf": (11, 3),
                 "f": (13, 0), "m4": (14, 3), "on2": (15, 0)}
        ACT_AT = {"o-1": (1, 1), "m1": (3, 0), "oT": (3, 1), "o0": (5, 0), "m2": (7, 0), "x1T": (9, 0),
                  "o1": (9, 0), "m3": (10, 1), "r": (11, 0), "kf": (12, 0), "o2": (13, 0),
                  "m4": (15, 0)}
        DVE_AT = {"on-1": (2, 0), "y": (3, 1), "y_stats0": (3, 1), "y_stats1": (3, 1), "on0": (5, 1),
                  "x1_stats0": (6, 1), "x1_stats1": (6, 1), "xr": (9, 1), "on1": (9, 1), "xk": (10, 1),
                  "gate0": (11, 0), "gate1": (11, 0), "gate2": (11, 1), "gate3": (12, 1), "f": (13, 1),
                  "f_stats0": (13, 1), "on2": (15, 0), "f_stats1": (15, 1)}
        JOBS.sort(key=lambda j: PE_AT[j[1]])

        def job_before(b, job, first, last):
            have = [j for j in JOBS if not (first and j[0] == "F") and not (last and j[0] == "L")]
            at = [j[1] for j in have].index(job)
            if not at:
                return (m_tak, 1) if first else (on_tak, b * NG - 1)
            _, _, taken, a, c = have[at - 1]
            return taken, b * a + c

        def later(n):
            return not isinstance(n, int) or n > 0

        TAIL = BLK - LEAD

        def score_bank(n, i, last):
            if last and n >= TAIL and i >= 2:
                return psA[:, 0, i - 2, :]
            return psB[:, i % 2, :]

        block = ctx.enter_context(nc.Block())

        @block.sync
        def _(sp):
            def load_x(b):
                sp.dma_start(x_all[:, b, :].rearrange("p (t c) -> p t c", t=NT),
                             x[b, :, :].rearrange("(t p) c -> p t c", p=P)).then_inc(s_xin[b], 16)

            load_x(0)
            for i, w in ((WQ, Wq), (WK, Wk), (WV, Wv), (WL, Wl)):
                sp.dma_start(w_in[:, i, :], w[:, :]).then_inc(s_w[i], 16)
            for i, v in ((V_BQ, bq), (V_BK, bk), (V_BV, bv), (V_BL, bl), (V_MR, mu_r), (V_MK, mu_k)):
                sp.dma_start(vec[:, i:i + 1], v.rearrange("(p a) -> p a", a=1)).then_inc(s_vec, 16)
            sp.dma_start(bo_row[:, :], bo.rearrange("(a n) -> a n", a=1)).then_inc(s_vec, 16)

            def write_part(b, i, scr, parts, made, written):
                sp.wait_ge(made, 2 * b + 2 if i == 0 else b + 1)
                sp.dma_start(scr[b, i, :, :, :].rearrange("d h n -> h d n"),
                             parts[:, b % 2, i, :]).then_inc(written[b], 16)

            def write_q(b, i):
                write_part(b, i, q_scr, qp, (q_tak, q_p1, q_p2)[i], q_wr)

            def write_k(b, i):
                write_part(b, i, k_scr, kp, (k_tak, k_p1, k_p2)[i], k_wr)

            def write_parts(b):
                for i in range(PARTS):
                    write_q(b, i)
                    write_k(b, i)

            def load_q(b, g):
                q_src = q_scr[ds(b, 1), :, :, GH * g:GH * (g + 1), :]
                for i in range(PARTS):
                    r = PARTS * D * i
                    sp.dma_start(QS[g][r:r + PARTS * D, :, :].rearrange("p h n -> p (h n)"),
                                 q_src[:, i:i + 1, :, :, :].rearrange("a i d h n -> a (i d) (h n)")
                                 .broadcast_to([PARTS, D, GH * T])).then_inc(ld[g], 16)

            def load_k(b, g):
                k_src = k_scr[ds(b, 1), :, :, GH * g:GH * (g + 1), :]
                sp.dma_start(KS[g][0:ROWS, :, :].rearrange("p h n -> p (h n)"),
                             k_src.rearrange("a i d h n -> a (i d) (h n)")
                             .broadcast_to([PARTS, PARTS * D, GH * T])).then_inc(ld[g], 16)

            def put_maxima(n, g):
                sp.wait_ge(m_tak, n + 1)
                sp.dma_start(QS[g][KMAX:KEXP, :, :].rearrange("p h n -> p (h n)"),
                             mmT[:, :]).then_inc(m_in, 16)

            def store(b):
                sp.wait_ge(out_rdy, b + 1)
                sp.dma_start(out[ds(b, 1), :, :].rearrange("a (t p) c -> (a p) t c", p=P),
                             out_sb[:, :, :]).then_inc(out_wr, 16)

            for b in range(1, NB):
                load_x(b)
            write_q(0, 0)
            write_k(0, 0)
            write_q(0, 1)
            write_q(0, 2)
            write_k(0, 1)
            write_k(0, 2)
            sp.wait_ge(q_wr[0], 16 * PARTS)
            for g in range(NG):
                sp.wait_ge(s_padp, (1, 4, 7, 10)[g])
                if g == 0:
                    sp.wait_ge(s_padv, 2)
                load_q(0, g)
                if g == 0:
                    sp.wait_ge(k_wr[0], 16 * PARTS)
                load_k(0, g)
            write_parts(1)
            put_maxima(0, 0)
            for b in range(2, NB):
                write_parts(b)
            for b in range(1, NB):
                sp.wait_ge(q_wr[b], 16 * PARTS)
                sp.wait_ge(k_wr[b], 16 * PARTS)

            def batch(b, first, last):
                for g in range(NG):
                    if g < NG - 1 or not last:
                        put_maxima(b * NG + (g + 1), (g + 1) % NG)
                    if not last:
                        sp.wait_ge(b_rdy, b * (BLK * GH) + GH * NT * (g + 1))
                        load_q(b + 1, g)
                        load_k(b + 1, g)
                if not first:
                    store(b - 1)

            batch(0, True, False)
            with sp.Fori(1, NB - 1) as i:
                batch(i, False, False)
            batch(NB - 1, False, True)
            for u in range(2):
                sp.wait_ge(z_out, u + 1)
                sp.dma_start(out[NB - 1, z_cols(u), :].rearrange("(t p) c -> p t c", p=P),
                             out_sb[:, HALF * u:HALF * (u + 1), :]).then_inc(z_wr, 16)
            sp.wait_ge(out_wr, 16 * (NB - 1))
            sp.wait_ge(z_wr, 16 * 2)

        @block.gpsimd
        def _(pool):
            steps = [0]

            def link(ins):
                steps[0] += 1
                ins.then_inc(s_const, 1)
                pool.wait_ge(s_const, steps[0])

            link(nc.gpsimd.memset(ident[:, :], 0.0))
            link(nc.gpsimd.affine_select(out=ident[:, :], in_=ident[:, :], compare_op=ALU.not_equal,
                                         fill=1.0, base=0, pattern=[[-1, P]], channel_multiplier=1))
            nc.gpsimd.tensor_copy(ident_b[:, :], ident[:, :]).then_inc(s_ident, 1)
            for dst, value in ((neghalf, -0.5), (eps, EPS), (one, 1.0), (minus, -1.0)):
                last = nc.gpsimd.memset(dst[:, :], value)
            link(last)

            def copy(dst, src, free):
                return nc.gpsimd.tensor_tensor(dst, src, one[:, :].broadcast_to([P, free]), ALU.mult)

            def rstd_x(b):
                pool.wait_ge(x_st, (b + 1) * (2 * NT))
                nc.gpsimd.tensor_tensor(ve_x[:, b, :], mv_x[:, b, :, 1], eps[:, :],
                                        ALU.add).then_inc(x_ve, 1)
                pool.wait_ge(x_ve, b + 1)
                nc.gpsimd.tensor_tensor(rs_x[:, b, :], ve_x[:, b, :], neghalf[:, :],
                                        ALU.pow).then_inc(x_rs, 1)

            def scale_and_shift(b, stats, mv, ve, rs, nm, nb, v_sem, r_sem, m_sem, b_sem):
                pool.wait_ge(stats, (b + 1) * (2 * NT))
                nc.gpsimd.tensor_tensor(ve[:, :], mv[:, :, 1], eps[:, :], ALU.add).then_inc(v_sem, 1)
                nc.gpsimd.tensor_tensor(nm[:, :], mv[:, :, 0], minus[:, :], ALU.mult).then_inc(m_sem, 1)
                pool.wait_ge(v_sem, b + 1)
                nc.gpsimd.tensor_tensor(rs[:, :], ve[:, :], neghalf[:, :], ALU.pow).then_inc(r_sem, 1)
                pool.wait_ge(m_sem, b + 1)
                pool.wait_ge(r_sem, b + 1)
                nc.gpsimd.tensor_tensor(nb[:, :], nm[:, :], rs[:, :], ALU.mult).then_inc(b_sem, 1)

            def split_qk(b):
                for full, rest, parts, taken, r1, p2 in ((qf, qr, qp, q_tak, q_r1, q_p2),
                                                         (kf, kr, kp, k_tak, k_r1, k_p2)):
                    pool.wait_ge(taken, b * 2 + 2)
                    pool.wait_ge(p2, b)
                    nc.gpsimd.tensor_tensor(rest[:, :], full[:, :], parts[:, b % 2, 0, :],
                                            ALU.subtract).then_inc(r1, 1)
                for rest, parts, p1, p2 in ((qr, qp, q_p1, q_p2), (kr, kp, k_p1, k_p2)):
                    pool.wait_ge(p1, b + 1)
                    nc.gpsimd.tensor_tensor(parts[:, b % 2, 2, :], rest[:, :], parts[:, b % 2, 1, :],
                                            ALU.subtract).then_inc(p2, 1)

            def v_group(b, g, first):
                if not first:
                    pool.wait_ge(pv_done, b * BLK + (NT * (g + 1) - BLK))
                v = v_st[:, ds(b, 1), :].rearrange("p a (t h d) -> p (a t) h d", t=NT, h=H)
                nc.gpsimd.tensor_tensor(Vg[:, g, :, :, 0:D], v[:, :, GH * g:GH * (g + 1), :],
                                        one[:, :].unsqueeze(2).unsqueeze(3).broadcast_to([P, NT, GH, D]),
                                        ALU.mult).then_inc(vg_rdy, 1)

            pads = [0]

            def pad(ap, value):
                pads[0] += 1
                nc.gpsimd.memset(ap.rearrange("p h n -> p (h n)").bitcast(u32), value)\
                    .then_inc(s_padp, 1)
                pool.wait_ge(s_padp, pads[0])

            def split_maxima(n, g):
                pool.wait_ge(a_max, (n + 1) * (2 * NT))
                if later(n):
                    pool.wait_ge(m_rdy, n)
                m, r = mx[:, g % 2, :], mr[:, g % 2, :]
                copy(mm[:, 0:MC], m, MC).then_inc(m_p0, 1)
                pool.wait_ge(m_p0, n + 1)
                nc.gpsimd.tensor_tensor(r, m, mm[:, 0:MC], ALU.subtract).then_inc(m_r1, 1)
                pool.wait_ge(m_r1, n + 1)
                copy(mm[:, MC:2 * MC], r, MC).then_inc(m_p1, 1)
                pool.wait_ge(m_p1, n + 1)
                nc.gpsimd.tensor_tensor(mm[:, 2 * MC:3 * MC], r, mm[:, MC:2 * MC],
                                        ALU.subtract).then_inc(m_p2, 1)

            pad(QS[0][64:KMAX, :, :], 0)
            rstd_x(0)
            link(nc.gpsimd.memset(mm[:, :], 0.0))
            link(nc.gpsimd.memset(ones_row[:, :], 1.0))
            for g in range(1, NG):
                pad(QS[g][64:KMAX, :, :], 0)
                pad(KS[g][64:KMAX, :, :], 0)
                pad(KS[g][KMAX:KEXP, :, :], MINUS_ONES)
                if g == 2:
                    rstd_x(1)
                    pool.wait_ge(x_rs, 2)
            link(nc.gpsimd.memset(Vg[:, :, :, :, :].rearrange("p g t h c -> p (g t h c)"), 0.0))
            link(nc.gpsimd.memset(Vg[:, :, :, :, D:D + 1], 1.0))
            link(nc.gpsimd.memset(xs[:, 0:1], 0.0))
            for b in range(2, NB):
                rstd_x(b)
            split_qk(1)
            pool.wait_ge(v_tak, 1)
            for g in range(NG):
                v_group(0, g, True)
            split_qk(2)
            split_maxima(0, 0)
            split_qk(3)

            def batch(b, first, last):
                if not first:
                    v_group(b, NG - 1, False)
                split_maxima(b * NG + 1, 1)
                if not first:
                    scale_and_shift(b - 1, y_st, mv_y, ve_y, rs_y, nm_y, nb_y, y_ve, y_rs, y_nm, y_nb)
                    normalise_rows(b - 1, ysb, zy, rs_y, nb_y, y_nb, y_z, x1_rdy)
                split_maxima(b * NG + 2, 2)
                if not first:
                    add_x(b - 1)
                if not last:
                    v_group(b + 1, 0, False)
                if not first:
                    scale_and_shift(b - 1, x1_st, mv_1, ve_1, rs_1, nm_1, nb_1, x1_ve, x1_rs, x1_nm,
                                    x1_nb)
                    normalise_rows(b - 1, x1, x1h, rs_1, nb_1, x1_nb, x1_h, None)
                    subtract_previous(b - 1)
                if not last:
                    v_group(b + 1, 1, False)
                split_maxima(b * NG + 3, 3)
                if not first:
                    add_one(b - 1)
                    square(b - 1)
                if not last:
                    v_group(b + 1, 2, False)
                    split_maxima(b * NG + 4, 0)
                if not first:
                    finish(b - 1)

            def normalise_rows(e, src, dst, rs, nb, shifts, done, before):
                pool.wait_ge(shifts, e + 1)
                if before is not None and later(e):
                    pool.wait_ge(before, e)
                nc.gpsimd.tensor_tensor(idle_p[:, :], one[:, :], one[:, :], ALU.mult)
                for t in range(NT):
                    last = nc.gpsimd.tensor_scalar(dst[:, t, :], src[:, t, :], rs[:, t:t + 1],
                                                   nb[:, t:t + 1], ALU.mult, ALU.add)
                last.then_inc(done, 1)

            def add_x(e):
                pool.wait_ge(y_z, e + 1)
                nc.gpsimd.tensor_tensor(x1[:, :, :].rearrange("p t c -> p (t c)"),
                                        x_all[:, ds(e, 1), :].rearrange("p a n -> p (a n)"),
                                        zy[:, :, :].rearrange("p t c -> p (t c)"),
                                        ALU.add).then_inc(x1_rdy, 1)

            def subtract_previous(e):
                pool.wait_ge(x1T_tak, e + 1)
                nc.gpsimd.tensor_tensor(dx[:, :], xs[:, 1:1 + T], xs[:, 0:T],
                                        ALU.subtract).then_inc(d_rdy, 1)

            def add_one(e):
                pool.wait_ge(r_tak, e + 1)
                nc.gpsimd.tensor_tensor(rr[:, :], er[:, :], one[:, :].broadcast_to([P, NT * E]),
                                        ALU.add).then_inc(r_add, 1)

            def square(e):
                pool.wait_ge(kf_tak, e + 1)
                nc.gpsimd.tensor_tensor(kact[:, :], krelu[:, :], krelu[:, :],
                                        ALU.mult).then_inc(ka_rdy, 1)

            def finish(e):
                scale_and_shift(e, f_st, mv_f, ve_f, rs_f, nm_f, nb_f, f_ve, f_rs, f_nm, f_nb)
                normalise_rows(e, f_sb, zf, rs_f, nb_f, f_nb, f_z, out_rdy)
                pool.wait_ge(f_z, e + 1)
                if later(e):
                    pool.wait_ge(out_wr, e * 16)
                nc.gpsimd.tensor_tensor(out_sb[:, :, :], x1[:, :, :], zf[:, :, :],
                                        ALU.add).then_inc(out_rdy, 1)

            batch(0, True, False)
            with pool.Fori(1, NB - 1) as i:
                batch(i, False, False)
            batch(NB - 1, False, True)

            def z_rstd(u, stats, mv, ve, rs, v_sem, r_sem):
                h = slice(HALF * u, HALF * (u + 1))
                pool.wait_ge(stats, 2 * HALF * (u + 1))
                nc.gpsimd.tensor_tensor(ve[:, h], mv[:, h, 1], eps[:, h], ALU.add).then_inc(v_sem, 1)
                pool.wait_ge(v_sem, u + 1)
                nc.gpsimd.tensor_tensor(rs[:, h], ve[:, h], neghalf[:, h], ALU.pow).then_inc(r_sem, 1)

            for u in range(2):
                z_rstd(u, z_yst, mv_y, ve_y, rs_y, z_yve, z_yrs)
            for u in range(2):
                z_rstd(u, z_1st, mv_1, ve_1, rs_1, z_1ve, z_1rs)
            for u in range(2):
                pool.wait_ge(z_relu, u + 1)
                nc.gpsimd.tensor_tensor(kact[:, z_cols(u)], krelu[:, z_cols(u)], krelu[:, z_cols(u)],
                                        ALU.mult).then_inc(z_ka, 1)
            for u in range(2):
                z_rstd(u, z_fst, mv_f, ve_f, rs_f, z_fve, z_frs)

        @block.scalar
        def _(act):
            for i, w in ((WO, Wo), (WR, W_r), (WKF, W_k), (WVF, W_v)):
                act.dma_start(w_in[:, i, :], w[:, :]).then_inc(s_w[i], 16)
            act.wait_ge(s_wt, 5)
            nc.scalar.copy(w_T[:, 0:4, :].rearrange("p a n -> p (a n)"), psA[:, 0, 0, :])\
                .then_inc(s_wtc, 1)
            nc.scalar.copy(w_T[:, 4, :], psA[:, 0, 1, 0:E]).then_inc(s_wtc, 1)

            def take_xT(b):
                act.wait_ge(xT_rdy, b + 1)
                if b >= 2:
                    act.wait_ge(v_rdy, b - 1)
                nc.scalar.copy(xhT[:, b % 2, :], psB[:, 0, :]).then_inc(xT_tak, 1)

            def take_parts(b, ps, full, parts, bias, ready, r1, taken, written):
                act.wait_ge(ready, b + 1)
                if b >= 1:
                    act.wait_ge(r1, b)
                if b >= 2:
                    act.wait_ge(written[b - 2], 16 * PARTS)
                nc.scalar.activation(full[:, :], ps[:, :], ACT.Identity, bias=bias).then_inc(taken, 1)
                nc.scalar.activation(parts[:, b % 2, 0, :], ps[:, :], ACT.Identity,
                                     bias=bias).then_inc(taken, 1)

            def take_q(b):
                take_parts(b, psO, qf, qp, vec[:, V_BQ:V_BQ + 1], q_rdy, q_r1, q_tak, q_wr)

            def take_k(b):
                take_parts(b, psM, kf, kp, b_kl[:, 0:1], k_rdy, k_r1, k_tak, k_wr)

            def second_part(b, rest, parts, r1, p1):
                act.wait_ge(r1, b + 1)
                nc.scalar.copy(parts[:, b % 2, 1, :], rest[:, :]).then_inc(p1, 1)

            def take_v(b):
                act.wait_ge(v_rdy, b + 1)
                nc.scalar.copy(v_st[:, b, :], psB[:, 1, :]).then_inc(v_tak, 1)

            take_xT(0)
            act.wait_ge(s_wkl, 2)
            nc.scalar.copy(w_kl[:, :, :].rearrange("p a n -> p (a n)"), psA[:, 1, 0, 0:2 * E])\
                .then_inc(s_wklc, 1)
            act.wait_ge(s_vec, 16 * 7)
            take_q(0)
            act.wait_ge(s_bklc, 2)
            take_k(0)
            take_v(0)
            def take_maxima(n, bank=psM_b):
                act.wait_ge(m_rdy, n + 1)
                if later(n):
                    act.wait_ge(m_in, n * 16)
                nc.scalar.copy(mmT[:, :], bank[0:PARTS * MC, 0:P]).then_inc(m_tak, 1)

            act.wait_ge(s_bo, 1)
            for t in range(NT):
                last = nc.scalar.copy(bout[:, t, :], psA[:, 1, 1, 0:E])
            last.then_inc(s_boc, 1)
            def take_first_maxima(_):
                take_maxima(0, psB[:, 0, :].bitcast(bf16))

            def second_q(b):
                second_part(b, qr, qp, q_r1, q_p1)

            def second_k(b):
                second_part(b, kr, kp, k_r1, k_p1)

            for take, b in ((take_xT, 1), (take_q, 1), (take_k, 1), (second_q, 1), (take_xT, 2),
                            (second_k, 1), (take_v, 1), (take_q, 2), (take_k, 2), (second_q, 2),
                            (take_xT, 3), (second_k, 2), (take_v, 2), (take_q, 3),
                            (take_first_maxima, 0), (take_k, 3), (take_v, 3), (second_q, 3),
                            (second_k, 3)):
                take(b)

            def take_o(n):
                act.wait_ge(pv_done, (n + 1) * NT)
                if later(n):
                    act.wait_ge(on_rdy, n)
                nc.scalar.copy(o_sb[:, :], psO[:, :]).then_inc(o_tak, 1)

            def take_oT(e):
                act.wait_ge(oT_rdy, e + 1)
                nc.scalar.copy(oT[:, :], psM[:, :]).then_inc(oT_tak, 1)

            def take_x1T(e):
                act.wait_ge(x1T_rdy, e + 1)
                nc.scalar.copy(xs[:, 1:1 + T], psM[:, :]).then_inc(x1T_tak, 1)

            def take_kf(e):
                act.wait_ge(kf_rdy, e + 1)
                nc.scalar.activation(krelu[:, :], psM[:, :], ACT.Relu).then_inc(kf_tak, 1)

            def take_r(e):
                act.wait_ge(r_rdy, e + 1)
                nc.scalar.activation(er[:, :], psM[:, :], ACT.Exp, scale=-1.0).then_inc(r_tak, 1)

            def exponentials(b, n, i, last):
                act.wait_ge(b_rdy, b * (BLK * GH) + (n * GH + i + 1))
                if n >= 2 or later(b):
                    act.wait_ge(pv_done, b * BLK + (n - 1))
                nc.scalar.activation(pT[:, n % 2, i, :], score_bank(n, i, last), ACT.Exp,
                                     scale=SCALE).then_inc(e_rdy, 1)

            def batch(b, first, last):
                for n in range(BLK):
                    take_results(b, n, 0, first, last)
                    exponentials(b, n, 0, last)
                    exponentials(b, n, 1, last)
                    take_results(b, n, 1, first, last)
                    exponentials(b, n, 2, last)
                    exponentials(b, n, 3, last)

            def take_results(b, n, half, first, last):
                here = [name for name in ACT_AT if ACT_AT[name] == (n, half)]
                for g in range(-1, NG - 1):
                    if f"o{g}" in here and not (g < 0 and first):
                        take_o(b * NG + g)
                for g in range(1, NG + 1):
                    if f"m{g}" in here and not (g == NG and last):
                        take_maxima(b * NG + g)
                if first:
                    return
                if "oT" in here:
                    take_oT(b - 1)
                if "x1T" in here:
                    take_x1T(b - 1)
                if "r" in here:
                    take_r(b - 1)
                if "kf" in here:
                    take_kf(b - 1)

            batch(0, True, False)
            with act.Fori(1, NB - 1) as i:
                batch(i, False, False)
            batch(NB - 1, False, True)

            for u in range(2):
                act.wait_ge(z_oT, u + 1)
                nc.scalar.copy(oT[:, z_cols(u)], z_bank["oT"][u][:, z_cols(u)]).then_inc(z_oTc, 1)

            def z_take_x1T(u):
                act.wait_ge(z_xT, u + 1)
                nc.scalar.copy(xs[:, 1 + HALF * P * u:1 + HALF * P * (u + 1)],
                               z_bank["x1T"][u][:, z_cols(u)]).then_inc(z_xs, 1)

            def z_take_r(u):
                act.wait_ge(z_r, u + 1)
                nc.scalar.activation(er[:, z_cols(u)], z_bank["r"][u][:, z_cols(u)], ACT.Exp,
                                     scale=-1.0).then_inc(z_er, 1)

            def z_add_one(u):
                act.wait_ge(z_er, u + 1)
                nc.scalar.activation(rr[:, z_cols(u)], er[:, z_cols(u)], ACT.Identity,
                                     bias=one[:, :]).then_inc(z_add, 1)

            def z_take_k(u):
                act.wait_ge(z_kf, u + 1)
                nc.scalar.activation(krelu[:, z_cols(u)], z_bank["kf"][u][:, z_cols(u)],
                                     ACT.Relu).then_inc(z_relu, 1)

            z_take_x1T(0)
            z_take_r(0)
            z_take_x1T(1)
            z_add_one(0)
            z_take_k(0)
            z_take_r(1)
            z_add_one(1)
            z_take_k(1)
            for u in range(2):
                act.wait_ge(z_fst, 2 * HALF * (u + 1))
                for t in z_tiles(u):
                    last = nc.scalar.activation(zf[:, t, :], f_sb[:, t, :], ACT.Identity, scale=-1.0,
                                                bias=mv_f[:, t, 0:1])
                last.then_inc(z_fc, 1)

        @block.vector
        def _(dve):
            def tile_stats(src, st, s, tiles):
                for t in tiles:
                    nc.vector.bn_stats(st[:, t, :], src(t)).then_inc(s[0], 1)

            def stats(src, st, mv, s, left=range(NT)):
                tile_stats(src, st, s, left)
                dve.wait_ge(s[0], s[1] * (2 * NT) + NT)
                nc.vector.memset(idle[:, :], 0.0)
                for t in range(NT):
                    nc.vector.bn_aggr(mv[:, t, :], st[:, t, :]).then_inc(s[0], 1)

            def x_stats(b):
                dve.wait_ge(s_xin[b], 16)
                stats(lambda t: x_all[:, b, E * t:E * (t + 1)], st_x[:, b, :, :], mv_x[:, b, :, :], (x_st, b))

            def x_normalise(b):
                dve.wait_ge(x_rs, b + 1)
                for t in range(NT):
                    last = nc.vector.tensor_scalar(xh[:, b, t, :], x_all[:, b, E * t:E * (t + 1)],
                                                   mv_x[:, b, t, 0:1], rs_x[:, b, t:t + 1],
                                                   ALU.subtract, ALU.mult)
                last.then_inc(x_h, 1)

            def split_first(full, rest, parts, taken, r1, p1, p2):
                dve.wait_ge(taken, 2)
                nc.vector.tensor_tensor(rest[:, :], full[:, :], parts[:, 0, 0, :],
                                        ALU.subtract).then_inc(r1, 1)
                dve.wait_ge(r1, 1)
                nc.vector.tensor_copy(parts[:, 0, 1, :], rest[:, :]).then_inc(p1, 1)
                dve.wait_ge(p1, 1)
                nc.vector.tensor_tensor(parts[:, 0, 2, :], rest[:, :], parts[:, 0, 1, :],
                                        ALU.subtract).then_inc(p2, 1)

            def pad(ap, value):
                nc.vector.memset(ap.rearrange("p h n -> p (h n)").bitcast(u32), value)\
                    .then_inc(s_padv, 1)

            nc.vector.memset(warm[:, :], 0.0).then_inc(s_warm, 1)
            x_stats(0)
            x_normalise(0)
            pad(KS[0][64:KMAX, :, :], 0)
            pad(KS[0][KMAX:KEXP, :, :], MINUS_ONES)
            dve.wait_ge(s_vec, 16 * 7)
            dve.wait_ge(s_bkl, 2)
            nc.vector.tensor_tensor(b_kl[:, 0:1], psA[:, 1, 1, 0:1], vec[:, V_BL:V_BL + 1],
                                    ALU.add).then_inc(s_bklc, 1)
            nc.vector.tensor_tensor(b_kl[:, 1:2], psA[:, 1, 1, 1:2], vec[:, V_BL:V_BL + 1],
                                    ALU.add).then_inc(s_bklc, 1)
            x_stats(1)
            split_first(qf, qr, qp, q_tak, q_r1, q_p1, q_p2)
            dve.wait_ge(s_bklc, 2)
            nc.vector.tensor_copy(bvl_wide[:, :], b_kl[:, 1:2].broadcast_to([P, P])).then_inc(s_wide, 1)
            split_first(kf, kr, kp, k_tak, k_r1, k_p1, k_p2)
            x_normalise(1)
            x_stats(2)
            x_stats(3)
            x_normalise(2)
            x_normalise(3)

            def maxima(group, a, g, h, u, free):
                dve.wait_ge(a_rdy, a * 2 + (u + 1))
                if h == 0 and u == 0 and free:
                    dve.wait_ge(m_p2, group - 1)
                c = NT * h + 2 * u
                nc.vector.tensor_reduce(out=mx[:, g % 2, c:c + 2], in_=psA[:, u, :, :],
                                        axis=AX.X, op=ALU.max).then_inc(a_max, 1)

            def normalise(n, g, oq_read):
                dve.wait_ge(on_rdy, n + 1)
                o = psM[:, :].rearrange("p (t h c) -> p t h c", t=NT, h=GH)
                nc.vector.reciprocal(rsum[:, :, :], o[:, :, :, D]).then_inc(o_rec, 1)
                dve.wait_ge(o_rec, n + 1)
                if oq_read is not None:
                    dve.wait_ge(oT_rdy, oq_read)
                nc.vector.tensor_tensor(oq[:, :, GH * g:GH * (g + 1), :], o[:, :, :, 0:D],
                                        rsum[:, :, :].unsqueeze(3).broadcast_to([P, NT, GH, D]),
                                        ALU.mult).then_inc(on_tak, 1)

            for a in range(LEAD):
                for u in range(2):
                    maxima(a // GH, a, a // GH, a % GH, u, False)

            def take_y(e):
                dve.wait_ge(y_rdy, e + 1)
                nc.vector.tensor_tensor(ysb[:, :, :].rearrange("p t c -> p (t c)"), psM[:, :],
                                        bout[:, :, :].rearrange("p t c -> p (t c)"),
                                        ALU.add).then_inc(y_tak, 1)
                dve.wait_ge(y_tak, e + 1)

            def y_stats(e, first):
                src, to = (lambda t: ysb[:, t, :]), (y_st, e)
                if first:
                    tile_stats(src, st_y, to, range(HALF))
                else:
                    stats(src, st_y, mv_y, to, range(HALF, NT))

            def x1_stats(e, first):
                src, to = (lambda t: x1[:, t, :]), (x1_st, e)
                if first:
                    dve.wait_ge(x1_rdy, e + 1)
                    tile_stats(src, st_1, to, range(HALF))
                else:
                    stats(src, st_1, mv_1, to, range(HALF, NT))

            def mix(e, dst, mu, s):
                dve.wait_ge(d_rdy, e + 1)
                nc.vector.scalar_tensor_tensor(out=dst[:, :], in0=dx[:, :], scalar=vec[:, mu:mu + 1],
                                               in1=xs[:, 0:T], op0=ALU.mult, op1=ALU.add).then_inc(s, 1)

            def take_f(e):
                dve.wait_ge(f_rdy, e + 1)
                dve.wait_ge(r_rec, (e + 1) * NT)
                nc.vector.tensor_tensor(f_sb[:, :, :].rearrange("p t c -> p (t c)"), psM[:, :],
                                        er[:, :], ALU.mult).then_inc(f_tak, 1)
                dve.wait_ge(f_tak, e + 1)

            def f_stats(e, first):
                src, to = (lambda t: f_sb[:, t, :]), (f_st, e)
                if first:
                    tile_stats(src, st_f, to, range(HALF))
                else:
                    stats(src, st_f, mv_f, to, range(HALF, NT))

            def sigmoid_part(e, t):
                dve.wait_ge(r_add, e + 1)
                nc.vector.reciprocal(er[:, E * t:E * (t + 1)], rr[:, E * t:E * (t + 1)])\
                    .then_inc(r_rec, 1)

            def batch(b, first, last):
                for n in range(BLK):
                    ahead = n + LEAD
                    g, h = ahead // GH % NG, ahead % GH
                    for u in range(2):
                        if ahead < BLK or not last:
                            maxima(b * NG + ahead // GH, b * BLK + ahead, g, h, u,
                                   u == 0 and (ahead >= 2 * GH or not first))
                        after_maxima(b, n, u, first)
                    if last and n == BLK - LEAD:
                        last_weights()

            def last_weights():
                for i, (mu, w) in enumerate(((V_MR, T_WR), (V_MK, T_WKF))):
                    nc.vector.tensor_scalar(w_mix[:, 2 * i, :], w_T[:, w, :], vec[:, mu:mu + 1], None,
                                            ALU.mult).then_inc(z_w, 1)
                nc.vector.tensor_scalar(w_mix[:, 4, :], w_T[:, T_WVF, :], -1.0, None,
                                        ALU.mult).then_inc(z_w, 1)
                rows = (w_in[:, WO, :], bout[:, 0, :])
                for i in range(2):
                    nc.vector.bn_stats(st_w[:, i, :], rows[i]).then_inc(z_c, 1)
                dve.wait_ge(z_w, 3)
                for i, w in enumerate((T_WR, T_WKF)):
                    nc.vector.tensor_tensor(w_mix[:, 2 * i + 1, :], w_T[:, w, :], w_mix[:, 2 * i, :],
                                            ALU.subtract).then_inc(z_w, 1)
                dve.wait_ge(z_c, 2)
                for i in range(2):
                    nc.vector.bn_aggr(mv_w[:, i, :], st_w[:, i, :]).then_inc(z_c, 1)
                dve.wait_ge(z_c, 4)
                for i in range(2):
                    nc.vector.tensor_scalar(w_cen[:, i, :], rows[i], mv_w[:, i, 0:1], None,
                                            ALU.subtract).then_inc(z_c, 1)

            def after_maxima(b, n, u, first):
                here = [name for name in DVE_AT if DVE_AT[name] == (n, u)]
                for g in range(-1, NG - 1):
                    if f"on{g}" in here and not (g < 0 and first):
                        normalise(b * NG + g, g % NG, b if g == 0 and not first else None)
                if first:
                    return
                e = b - 1
                if "y" in here:
                    take_y(e)
                for half in range(2):
                    if f"y_stats{half}" in here:
                        y_stats(e, half == 0)
                    if f"x1_stats{half}" in here:
                        x1_stats(e, half == 0)
                if "xr" in here:
                    mix(e, xr, V_MR, xr_rdy)
                if "xk" in here:
                    mix(e, xk, V_MK, xk_rdy)
                for t in range(NT):
                    if f"gate{t}" in here:
                        sigmoid_part(e, t)
                if "f" in here:
                    take_f(e)
                for half in range(2):
                    if f"f_stats{half}" in here:
                        f_stats(e, half == 0)

            batch(0, True, False)
            with dve.Fori(1, NB - 1) as i:
                batch(i, False, False)
            batch(NB - 1, False, True)

            e = NB - 1

            def z_normalise(u):
                dve.wait_ge(z_on, u + 1)
                h = slice(HALF * u, HALF * (u + 1))
                o = z_bank["on"][u][:, z_cols(u)].rearrange("p (t h c) -> p t h c", t=HALF, h=GH)
                nc.vector.reciprocal(rsum[:, h, :], o[:, :, :, D]).then_inc(z_rec, 1)
                dve.wait_ge(z_rec, u + 1)
                nc.vector.tensor_tensor(oq[:, h, GH * (NG - 1):H, :], o[:, :, :, 0:D],
                                        rsum[:, h, :].unsqueeze(3).broadcast_to([P, HALF, GH, D]),
                                        ALU.mult).then_inc(z_oq, 1)

            def z_stats(u, src, st, mv, s):
                for t in z_tiles(u):
                    nc.vector.bn_stats(st[:, t, :], src(t)).then_inc(s, 1)
                dve.wait_ge(s, 2 * HALF * u + HALF)
                for t in z_tiles(u):
                    nc.vector.bn_aggr(mv[:, t, :], st[:, t, :]).then_inc(s, 1)

            def z_y(u):
                return lambda t: z_bank["y"][u][:, E * t:E * (t + 1)]

            def z_take_y(u):
                dve.wait_ge(z_yp, u + 1)
                z_stats(u, z_y(u), st_y, mv_y, z_yst)

            def z_scale_add(u, src, rs, other, dst, scales, done):
                dve.wait_ge(scales, u + 1)
                for t in z_tiles(u):
                    last = nc.vector.scalar_tensor_tensor(out=dst[:, t, :], in0=src(t),
                                                          scalar=rs[:, t:t + 1], in1=other(t),
                                                          op0=ALU.mult, op1=ALU.add)
                last.then_inc(done, 1)

            def z_take_x1(u):
                z_scale_add(u, z_y(u), rs_y, lambda t: x_all[:, e, E * t:E * (t + 1)], x1, z_yrs, z_x1)
                dve.wait_ge(z_x1, u + 1)
                z_stats(u, lambda t: x1[:, t, :], st_1, mv_1, z_1st)

            def z_write(u):
                dve.wait_ge(z_fc, u + 1)
                z_scale_add(u, lambda t: zf[:, t, :], rs_f, lambda t: x1[:, t, :], out_sb, z_frs, z_out)

            def z_normalise_x1(u):
                dve.wait_ge(z_1rs, u + 1)
                for t in z_tiles(u):
                    last = nc.vector.tensor_scalar(x1h[:, t, :], x1[:, t, :], mv_1[:, t, 0:1],
                                                   rs_1[:, t:t + 1], ALU.subtract, ALU.mult)
                last.then_inc(z_1h, 1)

            def z_take_gate(u):
                dve.wait_ge(z_add, u + 1)
                nc.vector.reciprocal(er[:, z_cols(u)], rr[:, z_cols(u)]).then_inc(z_gate, 1)

            def z_take_f(u):
                dve.wait_ge(z_fp, u + 1)
                dve.wait_ge(z_gate, u + 1)
                h = slice(HALF * u, HALF * (u + 1))
                nc.vector.tensor_tensor(f_sb[:, h, :].rearrange("p t c -> p (t c)"),
                                        z_bank["f"][u][:, z_cols(u)], er[:, z_cols(u)],
                                        ALU.mult).then_inc(z_f, 1)
                dve.wait_ge(z_f, u + 1)
                z_stats(u, lambda t: f_sb[:, t, :], st_f, mv_f, z_fst)

            dve.wait_ge(pv_done, NB * BLK)
            for u in range(2):
                nc.vector.tensor_copy(o_sb[:, z_cols(u)], psO[:, z_cols(u)]).then_inc(z_o, 1)
            z_normalise(0)
            z_normalise(1)
            for step in (z_take_y, z_take_x1, z_normalise_x1, z_take_gate):
                step(0)
                step(1)
            z_take_f(0)
            z_take_f(1)
            dve.wait_ge(out_wr, 16 * (NB - 1))
            z_write(0)
            z_write(1)

        @block.tensor
        def _(pe):
            def keep_warm(count):
                for _ in range(count):
                    nc.tensor.matmul(psA[:, 1, 0, :], warm[:, 0:P], warm[:, :], start=True, stop=True)

            pe.wait_ge(s_warm, 1)
            keep_warm(9)
            pe.wait_ge(s_ident, 1)
            for j, i in ((T_WK, WK), (T_WV, WV), (T_WR, WR), (T_WKF, WKF), (T_WVF, WVF)):
                pe.wait_ge(s_w[i], 16)
                nc.tensor.transpose(psA[:, 0, j // 4, E * (j % 4):E * (j % 4 + 1)], w_in[:, i, :],
                                    ident[:, :]).then_inc(s_wt, 1)

            def product_by_tile(lhs, rhs, ready):
                for t in range(NT):
                    last = nc.tensor.matmul(psM[:, E * t:E * (t + 1)], lhs[:, P * t:P * (t + 1)], rhs,
                                            start=True, stop=True)
                last.then_inc(ready, 1)

            def transposes(src, ready):
                for t in range(NT):
                    last = nc.tensor.transpose(psM[:, P * t:P * (t + 1)], src(t), ident[:, :])
                last.then_inc(ready, 1)

            def job_xT(e):
                pe.wait_ge(x_h, e + 1)
                for t in range(NT):
                    last = nc.tensor.transpose(psB[:, 0, P * t:P * (t + 1)], xh[:, e, t, :], ident[:, :])
                last.then_inc(xT_rdy, 1)

            def job_q(e):
                pe.wait_ge(xT_tak, e + 1)
                if e:
                    pe.wait_ge(q_tak, 2 * e)
                nc.tensor.matmul(psO[:, :], w_in[:, WQ, :], xhT[:, e % 2, :], start=True, stop=True)\
                    .then_inc(q_rdy, 1)

            def job_k(e):
                if e:
                    pe.wait_ge(k_tak, 2 * e)
                nc.tensor.matmul(psM[:, :], w_kl[:, 0, :], xhT[:, e % 2, :], start=True, stop=True)\
                    .then_inc(k_rdy, 1)

            def job_v(e):
                if e:
                    pe.wait_ge(v_tak, e)
                for t in range(NT):
                    last = nc.tensor.matmul(psB[:, 1, E * t:E * (t + 1)], xhT[:, e % 2, P * t:P * (t + 1)],
                                            w_kl[:, 1, :], start=True, stop=True)
                last.then_inc(v_rdy, 1)

            def job_m(n, bank=psM_b):
                pe.wait_ge(m_p2, n + 1)
                nc.tensor.transpose(bank[:, 0:P], mm[:, :], ident_b[:, :]).then_inc(m_rdy, 1)

            def job_on(n):
                pe.wait_ge(o_tak, n + 1)
                transposes(lambda t: o_sb[:, P * t:P * (t + 1)], on_rdy)

            def job_oT(e):
                pe.wait_ge(on_tak, (e + 1) * NG)
                transposes(lambda t: oq[:, t, :, :].rearrange("p h d -> p (h d)"), oT_rdy)

            def job_y(e):
                pe.wait_ge(oT_tak, e + 1)
                product_by_tile(oT, w_in[:, WO, :], y_rdy)

            def job_x1T(e):
                pe.wait_ge(x1_h, e + 1)
                transposes(lambda t: x1h[:, t, :], x1T_rdy)

            def job_kf(e):
                pe.wait_ge(xk_rdy, e + 1)
                nc.tensor.matmul(psM[:, :], w_T[:, T_WKF, :], xk[:, :], start=True, stop=True)\
                    .then_inc(kf_rdy, 1)

            def job_r(e):
                pe.wait_ge(xr_rdy, e + 1)
                product_by_tile(xr, w_T[:, T_WR, :], r_rdy)

            def job_f(e):
                pe.wait_ge(ka_rdy, e + 1)
                product_by_tile(kact, w_T[:, T_WVF, :], f_rdy)

            def scores_for_maxima(e, a, g, h, u, j, free=False):
                if u == 0 and j == 0 and h == 0:
                    pe.wait_ge(ld[g], (e + 1) * (16 * LW))
                if j == 0 and not free:
                    pe.wait_ge(a_max, a * 2 + (u - 1))
                t = 2 * u + j
                score = nc.tensor.matmul(psA[:, u, j, :], QS[g][0:KMAX, h, P * t:P * (t + 1)],
                                         KS[g][0:KMAX, h, :], start=True, stop=True)
                if j == 1:
                    score.then_inc(a_rdy, 1)

            def scores_for_exponentials(b, n, i, later_tile, last):
                g, t = n // NT, n % NT
                if t == 0 and i == 0:
                    pe.wait_ge(m_in, b * (16 * NG) + 16 * (g + 1))
                if last and n >= TAIL and i >= 2 and n == TAIL:
                    if i == 2:
                        pe.wait_ge(a_max, 2 * BLK * NB)
                elif last and (n > TAIL or n == TAIL and i >= 2):
                    pe.wait_ge(e_rdy, b * (BLK * GH) + (n * GH + i - 3))
                elif later_tile:
                    pe.wait_ge(e_rdy, b * (BLK * GH) + (n * GH + i - 1))
                nc.tensor.matmul(score_bank(n, i, last), KS[g][0:KEXP, i, P * t:P * (t + 1)],
                                 QS[g][0:KEXP, i, :], start=True, stop=True).then_inc(b_rdy, 1)

            def times_v(b, n, later_group):
                g, t = n // NT % NG, n % NT
                if t == 0:
                    pe.wait_ge(vg_rdy, b * NG + (n // NT + 1))
                    if later_group:
                        pe.wait_ge(o_tak, b * NG + n // NT)
                pe.wait_ge(e_rdy, b * (BLK * GH) + GH * (n + 1))
                for i in range(GH):
                    last = nc.tensor.matmul(psO[QUAD * i:QUAD * (i + 1), :], Vg[:, g, t, i, :],
                                            pT[:, n % 2, i, :], start=(t == 0), stop=(t == NT - 1))
                last.then_inc(pv_done, 1)

            job_xT(0)
            pe.wait_ge(s_wtc, 2)
            pe.wait_ge(s_w[WL], 16)
            for j in range(2):
                nc.tensor.matmul(psA[:, 1, 0, E * j:E * (j + 1)], w_T[:, T_WK + j, :], w_in[:, WL, :],
                                 start=True, stop=True).then_inc(s_wkl, 1)
            job_q(0)
            pe.wait_ge(s_vec, 16 * 7)
            for j in range(2):
                nc.tensor.matmul(psA[:, 1, 1, j:j + 1], w_in[:, WL, :], vec[:, V_BK + j:V_BK + j + 1],
                                 start=True, stop=True).then_inc(s_bkl, 1)
            pe.wait_ge(s_wklc, 1)
            job_k(0)
            job_v(0)
            pe.wait_ge(s_wide, 1)
            pe.wait_ge(s_w[WO], 16)
            pe.wait_ge(s_const, 5)
            nc.tensor.matmul(psA[:, 1, 1, 0:E], bvl_wide[:, :], w_in[:, WO, :], start=True, stop=False)
            nc.tensor.matmul(psA[:, 1, 1, 0:E], ones_row[:, :], bo_row[:, :], start=False,
                             stop=True).then_inc(s_bo, 1)
            keep_warm(8)
            job_xT(1)
            job_q(1)
            job_k(1)
            LEAD_JOBS = {(0, 0): (("xT", 2), ("v", 1),),
                         (1, 0): (("q", 2),),
                         (1, 1): (("k", 2),),
                         (2, 0): (("v", 2),),
                         (2, 1): (("xT", 3),),
                         (4, 0): (("q", 3), ("k", 3),),
                         (5, 0): (("v", 3),)}
            for a in range(LEAD):
                for u in range(2):
                    if a == 0 and u == 1:
                        pe.wait_ge(s_boc, 1)
                    if a == GH and u == 1:
                        pe.wait_ge(xT_tak, NB)
                        job_m(0, psB[:, 0, :].bitcast(bf16))
                    for j in range(2):
                        scores_for_maxima(0, a, a // GH, a % GH, u, j, a == 0)
                    for job, e in LEAD_JOBS.get((a, u), ()):
                        {"xT": job_xT, "q": job_q, "k": job_k, "v": job_v}[job](e)
            pe.wait_ge(v_tak, NB)
            pe.wait_ge(m_tak, 1)

            def batch(b, first, last):
                def jobs(n, place):
                    for kind, name, _, _, _ in JOBS:
                        if PE_AT[name] == (n, place) and not (first and kind == "F") \
                                and not (last and kind == "L"):
                            pe.wait_ge(*job_before(b, name, first, last))
                            run_job(name)

                def run_job(name):
                    if name.startswith("on"):
                        job_on(b * NG + int(name[2:]))
                    elif name.startswith("m"):
                        job_m(b * NG + int(name[1:]))
                    else:
                        {"oT": job_oT, "y": job_y, "x1T": job_x1T, "r": job_r, "kf": job_kf,
                         "f": job_f}[name](b - 1)

                for n in range(BLK):
                    ahead = n + LEAD

                    def for_maxima(u, j):
                        if ahead < BLK or not last:
                            scores_for_maxima(b + ahead // BLK, b * BLK + ahead, ahead // GH % NG,
                                              ahead % GH, u, j)

                    def for_exponentials(i):
                        scores_for_exponentials(b, n, i, i > 1 or n > 0 or not first, last)

                    for_exponentials(0)
                    for_maxima(0, 0)
                    for_exponentials(1)
                    for_maxima(0, 1)
                    jobs(n, 0)
                    for_maxima(1, 0)
                    jobs(n, 1)
                    for_exponentials(2)
                    for_maxima(1, 1)
                    jobs(n, 2)
                    for_exponentials(3)
                    if first and n == 0:
                        pe.wait_ge(k_tak, 2 * NB)
                        pe.wait_ge(q_tak, 2 * NB)
                    jobs(n, 3)
                    if n or not first:
                        times_v_before(b, n, first)
                    jobs(n, 4)

            def times_v_before(b, n, first):
                if n:
                    times_v(b, n - 1, n > 1 or not first)
                else:
                    times_v(b - 1, BLK - 1, True)

            batch(0, True, False)
            with pe.Fori(1, NB - 1) as i:
                batch(i, False, False)
            batch(NB - 1, False, True)
            e = NB - 1
            times_v(e, BLK - 1, True)

            def z_transposes(u, bank, src, ready):
                for t in z_tiles(u):
                    last = nc.tensor.transpose(z_bank[bank][u][:, P * t:P * (t + 1)], src(t), ident[:, :])
                last.then_inc(ready, 1)

            def z_product_by_tile(u, bank, *terms, ready):
                for t in z_tiles(u):
                    for i, (lhs, rhs) in enumerate(terms):
                        last = nc.tensor.matmul(z_bank[bank][u][:, E * t:E * (t + 1)], lhs(t), rhs,
                                                start=(i == 0), stop=(i == len(terms) - 1))
                last.then_inc(ready, 1)

            for u in range(2):
                pe.wait_ge(z_o, u + 1)
                z_transposes(u, "on", lambda t: o_sb[:, P * t:P * (t + 1)], z_on)
            for u in range(2):
                pe.wait_ge(z_oq, u + 1)
                z_transposes(u, "oT", lambda t: oq[:, t, :, :].rearrange("p h d -> p (h d)"), z_oT)
            pe.wait_ge(z_c, 6)
            for u in range(2):
                pe.wait_ge(z_oTc, u + 1)
                z_product_by_tile(u, "y", (lambda t: oT[:, P * t:P * (t + 1)], w_cen[:, 0, :]),
                                  (lambda t: ones_row[:, :], w_cen[0:1, 1, :]), ready=z_yp)
            keep_warm(19)

            def z_x1T(u):
                pe.wait_ge(z_1h, u + 1)
                z_transposes(u, "x1T", lambda t: x1h[:, t, :], z_xT)

            def z_product_r(u):
                pe.wait_ge(z_xs, u + 1)
                z_product_by_tile(u, "r", (lambda t: xs[:, 1 + P * t:1 + P * (t + 1)], w_mix[:, 0, :]),
                                  (lambda t: xs[:, P * t:P * (t + 1)], w_mix[:, 1, :]), ready=z_r)

            def z_product_k(u):
                for i in range(2):
                    c = HALF * P * u + (1 - i)
                    last = nc.tensor.matmul(z_bank["kf"][u][:, z_cols(u)], w_mix[:, 2 + i, :],
                                            xs[:, c:c + HALF * P], start=(i == 0), stop=(i == 1))
                last.then_inc(z_kf, 1)

            z_x1T(0)
            pe.wait_ge(z_w, 5)
            z_product_r(0)
            z_x1T(1)
            z_product_k(0)
            z_product_r(1)
            z_product_k(1)
            for u in range(2):
                pe.wait_ge(z_ka, u + 1)
                z_product_by_tile(u, "f", (lambda t: kact[:, P * t:P * (t + 1)], w_mix[:, 4, :]),
                                  ready=z_fp)


_INS = ["x", "Wq", "bq", "Wk", "bk", "Wv", "bv", "Wl", "bl", "Wo", "bo"]
_FFN = ["W_r", "W_k", "W_v", "mu_r", "mu_k"]


def kernel(**inputs):
    import numpy as _np
    import concourse.bacc as _bacc
    from concourse import mybir as _mybir
    from concourse.bass_utils import run_bass_kernel_spmd as _run

    nc = _bacc.Bacc("TRN2", target_bir_lowering=False, num_devices=1)
    arrays, args = {}, []
    for name in ["L0_attn_" + n for n in _INS] + ["L0_ffn_" + n for n in _FFN]:
        a = _np.ascontiguousarray(inputs[name])
        arrays[f"in_{name}_dram"] = a
        args.append(nc.dram_tensor(f"in_{name}_dram", a.shape, _mybir.dt.from_np(a.dtype),
                                   kind="ExternalInput").ap())
    shape = inputs["L0_attn_x"].shape
    args.append(nc.dram_tensor("out_dram", shape, _mybir.dt.float32, kind="ExternalOutput").ap())
    sandwich_kernel(nc, *args)
    r = _run(nc, [arrays], core_ids=[0])
    return r.results[0]["out_dram"]
```
